# Optimizing a Trainium2 kernel written in Bass

```python
import numpy as np
import jax
import jax.numpy as jnp

def _softmax(x, axis=-1):
    return jax.nn.softmax(x, axis=axis)

def _gelu(x):
    return jax.nn.gelu(x, approximate=True)

def _silu(x):
    return jax.nn.silu(x)

def _sigmoid(x):
    return jax.nn.sigmoid(x)

def _layernorm(x, axis=-1, eps=1e-05):
    m = jnp.mean(x, axis=axis, keepdims=True)
    v = jnp.var(x, axis=axis, keepdims=True)
    return (x - m) / jnp.sqrt(v + eps)

def _scatter_add(tgt, idx, src, axis=0):
    return tgt.at[idx].add(src)

def _segment_sum(src, seg, n):
    return jax.ops.segment_sum(src, seg, n)
kernel_name = 'mk_gnn_preln_d2_gnn_r8_e932bb'

def setup_inputs(seed: int=0):
    np.random.seed(seed)
    _w = jnp.asarray

    def _rec_inputs():
        import jax
        import jax.numpy as jnp
        _gk = jax.random.key(seed)
        x = -0.000202 + 1 * jax.random.normal(jax.random.fold_in(_gk, 1), (6250, 128), jnp.float32)
        _s = jax.random.randint(jax.random.fold_in(_gk, 2), (50000,), 0, 6250, jnp.int32)
        _d = jax.random.randint(jax.random.fold_in(_gk, 3), (50000,), 0, 6250, jnp.int32)
        _loop = jnp.arange(6250, dtype=jnp.int32)
        src = jnp.concatenate([_s, _d, _loop])
        dst = jnp.concatenate([_d, _s, _loop])
        _o = jnp.argsort(dst, stable=True)
        src = src[_o]
        dst = dst[_o]
        edge_attr_64 = -8.62073e-06 + 0.999901 * jax.random.normal(jax.random.fold_in(_gk, 12), (106250, 64), jnp.float32)
        edge_type_4 = jax.random.randint(jax.random.fold_in(_gk, 14), (106250,), 0, 4, jnp.int32)
        return (x, src, dst, edge_attr_64, edge_type_4)
    x, src, dst, edge_attr_64, edge_type_4 = _rec_inputs()

    def _L0_gnn_setup():
        import jax, jax.numpy as jnp
        import numpy as np
        N = 6250
        E = 100000
        IN = 128
        OUT = 128
        R = 4
        H = 8
        D = OUT // H
        NEG_SLOPE = 0.2

        def _hgnn_forward(node_inp, edge_index, edge_type, W_rel, att_src_rel, att_dst_rel, bias_rel, W_self, W_cross, att_src_lang, att_dst_lang, bias_lang):
            src, dst = (edge_index[0], edge_index[1])

            def rel_gat(W, a_s, a_d, b, mask):
                x = (node_inp @ W).reshape(N, H, D)
                es = jnp.einsum('nhd,hd->nh', x, a_s)
                ed = jnp.einsum('nhd,hd->nh', x, a_d)
                logit = jax.nn.leaky_relu(es[src] + ed[dst], NEG_SLOPE)
                logit = jnp.where(mask[:, None], logit, -1e+30)
                mx = jax.ops.segment_max(logit, dst, num_segments=N)
                mx = jnp.maximum(mx, -1e+30)
                p = jnp.exp(logit - mx[dst]) * mask[:, None]
                den = jax.ops.segment_sum(p, dst, num_segments=N)
                alpha = p / jnp.where(den > 0, den, 1.0)[dst]
                msg = alpha[..., None] * x[src]
                out = jax.ops.segment_sum(msg, dst, num_segments=N)
                tmask = jax.ops.segment_sum(mask.astype(jnp.float32), dst, num_segments=N) > 0
                return (out.reshape(N, OUT) + b, tmask)
            rel_masks = edge_type[None, :] == jnp.arange(R)[:, None]
            rel_out, tmask = jax.vmap(rel_gat)(W_rel, att_src_rel, att_dst_rel, bias_rel, rel_masks)
            h = jax.nn.gelu(rel_out, approximate=False) @ W_cross
            S = node_inp @ W_self
            ent = jnp.concatenate([S[None], h], axis=0).reshape(R + 1, N, H, D)
            valid = jnp.concatenate([jnp.ones((1, N), bool), tmask], axis=0)
            ls = jnp.einsum('knhd,hd->knh', ent, att_src_lang)
            ld = jnp.einsum('nhd,hd->nh', ent[0], att_dst_lang)
            logit = jax.nn.leaky_relu(ls + ld[None], NEG_SLOPE)
            logit = jnp.where(valid[..., None], logit, -jnp.inf)
            alpha = jax.nn.softmax(logit, axis=0)
            out = jnp.einsum('knh,knhd->nhd', alpha, ent).reshape(N, OUT)
            return out + bias_lang
        key = jax.random.key(seed)
        ks = jax.random.split(key, 12)
        s = 0.05
        return {'node_inp': jax.random.normal(ks[0], (N, IN), dtype=jnp.float32), 'edge_index': jax.random.randint(ks[1], (2, E), 0, N), 'edge_type': jax.random.randint(ks[2], (E,), 0, R), 'W_rel': jax.random.normal(ks[3], (R, IN, OUT), dtype=jnp.float32) * s, 'att_src_rel': jax.random.normal(ks[4], (R, H, D), dtype=jnp.float32) * s, 'att_dst_rel': jax.random.normal(ks[5], (R, H, D), dtype=jnp.float32) * s, 'bias_rel': jax.random.normal(ks[6], (R, OUT), dtype=jnp.float32) * s, 'W_self': jax.random.normal(ks[7], (IN, OUT), dtype=jnp.float32) * s, 'W_cross': jax.random.normal(ks[8], (OUT, OUT), dtype=jnp.float32) * s, 'att_src_lang': jax.random.normal(ks[9], (H, D), dtype=jnp.float32) * s, 'att_dst_lang': jax.random.normal(ks[10], (H, D), dtype=jnp.float32) * s, 'bias_lang': jax.random.normal(ks[11], (OUT,), dtype=jnp.float32) * s}
    _L0_gnn_all = _L0_gnn_setup()
    _L0_gnn_in = {k: v for k, v in _L0_gnn_all.items() if k in ('W_rel', 'att_src_rel', 'att_dst_rel', 'bias_rel', 'W_self', 'W_cross', 'att_src_lang', 'att_dst_lang', 'bias_lang')}
    del _L0_gnn_all

    def _L1_gnn_setup():
        import jax, jax.numpy as jnp
        import numpy as np
        NEG_SLOPE = 0.01
        N_NODES = 12500
        N_EDGES = 62500
        IN_DIM, OUT_DIM, EF_DIM, EMB_DIM = (128, 128, 64, 256)

        def leaky_relu(x):
            return jnp.where(x >= 0, x, NEG_SLOPE * x)
        key = jax.random.key(seed)
        ks = jax.random.split(key, 8)
        s = 0.05
        nf = jax.random.normal(ks[0], (N_NODES, IN_DIM), dtype=jnp.float32)
        ef = jax.random.normal(ks[1], (N_EDGES, EF_DIM), dtype=jnp.float32)
        src = jax.random.randint(ks[2], (N_EDGES,), 0, N_NODES, dtype=jnp.int32)
        dst = jax.random.randint(ks[3], (N_EDGES,), 0, N_NODES, dtype=jnp.int32)
        We1 = jax.random.normal(ks[4], (2 * IN_DIM + EF_DIM, EMB_DIM), dtype=jnp.float32) * s
        We2 = jax.random.normal(ks[5], (EMB_DIM, OUT_DIM), dtype=jnp.float32) * s
        Wn1 = jax.random.normal(ks[6], (IN_DIM + OUT_DIM, EMB_DIM), dtype=jnp.float32) * s
        Wn2 = jax.random.normal(ks[7], (EMB_DIM, OUT_DIM), dtype=jnp.float32) * s
        return {'nf': nf, 'ef': ef, 'src': src, 'dst': dst, 'We1': We1, 'We2': We2, 'Wn1': Wn1, 'Wn2': Wn2}
    _L1_gnn_all = _L1_gnn_setup()
    _L1_gnn_in = {k: v for k, v in _L1_gnn_all.items() if k in ('We1', 'We2', 'Wn1', 'Wn2')}
    del _L1_gnn_all
    return {'x': x, 'src': src, 'dst': dst, 'edge_attr_64': edge_attr_64, 'edge_type_4': edge_type_4, 'L0_gnn_W_rel': _L0_gnn_in['W_rel'], 'L0_gnn_att_src_rel': _L0_gnn_in['att_src_rel'], 'L0_gnn_att_dst_rel': _L0_gnn_in['att_dst_rel'], 'L0_gnn_bias_rel': _L0_gnn_in['bias_rel'], 'L0_gnn_W_self': _L0_gnn_in['W_self'], 'L0_gnn_W_cross': _L0_gnn_in['W_cross'], 'L0_gnn_att_src_lang': _L0_gnn_in['att_src_lang'], 'L0_gnn_att_dst_lang': _L0_gnn_in['att_dst_lang'], 'L0_gnn_bias_lang': _L0_gnn_in['bias_lang'], 'L1_gnn_We1': _L1_gnn_in['We1'], 'L1_gnn_We2': _L1_gnn_in['We2'], 'L1_gnn_Wn1': _L1_gnn_in['Wn1'], 'L1_gnn_Wn2': _L1_gnn_in['Wn2']}

def reference(x, src, dst, edge_attr_64, edge_type_4, L0_gnn_W_rel, L0_gnn_att_src_rel, L0_gnn_att_dst_rel, L0_gnn_bias_rel, L0_gnn_W_self, L0_gnn_W_cross, L0_gnn_att_src_lang, L0_gnn_att_dst_lang, L0_gnn_bias_lang, L1_gnn_We1, L1_gnn_We2, L1_gnn_Wn1, L1_gnn_Wn2):
    import jax
    import jax.numpy as jnp

    def _L0_gnn_ref(node_inp, edge_index, edge_type, W_rel, att_src_rel, att_dst_rel, bias_rel, W_self, W_cross, att_src_lang, att_dst_lang, bias_lang):
        import jax, jax.numpy as jnp
        import numpy as np
        N = 6250
        E = 100000
        IN = 128
        OUT = 128
        R = 4
        H = 8
        D = OUT // H
        NEG_SLOPE = 0.2

        def _hgnn_forward(node_inp, edge_index, edge_type, W_rel, att_src_rel, att_dst_rel, bias_rel, W_self, W_cross, att_src_lang, att_dst_lang, bias_lang):
            src, dst = (edge_index[0], edge_index[1])

            def rel_gat(W, a_s, a_d, b, mask):
                x = (node_inp @ W).reshape(N, H, D)
                es = jnp.einsum('nhd,hd->nh', x, a_s)
                ed = jnp.einsum('nhd,hd->nh', x, a_d)
                logit = jax.nn.leaky_relu(es[src] + ed[dst], NEG_SLOPE)
                logit = jnp.where(mask[:, None], logit, -1e+30)
                mx = jax.ops.segment_max(logit, dst, num_segments=N)
                mx = jnp.maximum(mx, -1e+30)
                p = jnp.exp(logit - mx[dst]) * mask[:, None]
                den = jax.ops.segment_sum(p, dst, num_segments=N)
                alpha = p / jnp.where(den > 0, den, 1.0)[dst]
                msg = alpha[..., None] * x[src]
                out = jax.ops.segment_sum(msg, dst, num_segments=N)
                tmask = jax.ops.segment_sum(mask.astype(jnp.float32), dst, num_segments=N) > 0
                return (out.reshape(N, OUT) + b, tmask)
            rel_masks = edge_type[None, :] == jnp.arange(R)[:, None]
            rel_out, tmask = jax.vmap(rel_gat)(W_rel, att_src_rel, att_dst_rel, bias_rel, rel_masks)
            h = jax.nn.gelu(rel_out, approximate=False) @ W_cross
            S = node_inp @ W_self
            ent = jnp.concatenate([S[None], h], axis=0).reshape(R + 1, N, H, D)
            valid = jnp.concatenate([jnp.ones((1, N), bool), tmask], axis=0)
            ls = jnp.einsum('knhd,hd->knh', ent, att_src_lang)
            ld = jnp.einsum('nhd,hd->nh', ent[0], att_dst_lang)
            logit = jax.nn.leaky_relu(ls + ld[None], NEG_SLOPE)
            logit = jnp.where(valid[..., None], logit, -jnp.inf)
            alpha = jax.nn.softmax(logit, axis=0)
            out = jnp.einsum('knh,knhd->nhd', alpha, ent).reshape(N, OUT)
            return out + bias_lang
        return _hgnn_forward(node_inp, edge_index, edge_type, W_rel, att_src_rel, att_dst_rel, bias_rel, W_self, W_cross, att_src_lang, att_dst_lang, bias_lang)

    def _L1_gnn_ref(nf, ef, src, dst, We1, We2, Wn1, Wn2):
        import jax, jax.numpy as jnp
        import numpy as np
        NEG_SLOPE = 0.01
        N_NODES = 12500
        N_EDGES = 62500
        IN_DIM, OUT_DIM, EF_DIM, EMB_DIM = (128, 128, 64, 256)

        def leaky_relu(x):
            return jnp.where(x >= 0, x, NEG_SLOPE * x)
        src_full = jnp.concatenate([src, dst])
        dst_full = jnp.concatenate([dst, src])
        ef_full = jnp.concatenate([ef, ef], axis=0)
        edge_in = jnp.concatenate([nf[src_full], nf[dst_full], ef_full], axis=-1)
        msg = leaky_relu(edge_in @ We1) @ We2
        red = jax.ops.segment_sum(msg, dst_full, num_segments=nf.shape[0])
        node_in = jnp.concatenate([nf, red], axis=-1)
        out_nf = leaky_relu(node_in @ Wn1) @ Wn2
        return out_nf
    edge_index = jnp.stack([src, dst])
    h = jnp.maximum(_layernorm(x, axis=-1), 0.0)
    x = x + _L0_gnn_ref(h, edge_index, edge_type_4, L0_gnn_W_rel, L0_gnn_att_src_rel, L0_gnn_att_dst_rel, L0_gnn_bias_rel, L0_gnn_W_self, L0_gnn_W_cross, L0_gnn_att_src_lang, L0_gnn_att_dst_lang, L0_gnn_bias_lang)
    h = jnp.maximum(_layernorm(x, axis=-1), 0.0)
    x = x + _L1_gnn_ref(h, edge_attr_64, src, dst, L1_gnn_We1, L1_gnn_We2, L1_gnn_Wn1, L1_gnn_Wn2)
    return x

_drawn_inputs = setup_inputs


def setup_inputs(seed=0):
    import zlib

    import numpy as np

    out = dict(_drawn_inputs(seed))
    spreads = {}
    factors = {'L0_gnn_att_src_rel': 181.343,
     'L0_gnn_att_dst_rel': 200.0,
     'L0_gnn_bias_rel': 8.0,
     'L0_gnn_att_src_lang': 8.0,
     'L0_gnn_att_dst_lang': 101.879}
    for name, (base, spread) in spreads.items():
        noise = np.random.default_rng([zlib.crc32(name.encode()), seed]).standard_normal(out[name].shape)
        drawn = base * np.exp(spread * noise) if base else spread * noise
        out[name] = jnp.asarray(drawn.astype(out[name].dtype))
    for name, factor in factors.items():
        out[name] = (out[name] * factor).astype(out[name].dtype)
    return out
```

```python
import concourse.bass as bass
from concourse import mybir
from contextlib import ExitStack

F32, I32, BF16 = mybir.dt.float32, mybir.dt.int32, mybir.dt.bfloat16
ALU = mybir.AluOpType
ACT = mybir.ActivationFunctionType
AX = mybir.AxisListType
ds = bass.ds

P = 128
N_NODES, N_EDGES = 6250, 106250
C = 128
R, H, D = 4, 8, 16
EF = 64
HID = 256
XR = C + H
TILES = 50
NP = TILES * P
WIN = 64
WINDOWS = -(-N_NODES // WIN)
WSLOTS = NP // WIN
G = 8
STEPS = -(-((N_EDGES + (P - 1) * WINDOWS) // P) // (2 * G)) * (2 * G)
DCOLS = -(-N_EDGES // P)
EPAD = DCOLS * P + 2 * P
SUM_ROWS = -(-(NP + P) // (4 * P)) * (4 * P)
KC = 8
PAD_DST = 1 << 20
BIG = 1e30
SLOPE0, SLOPE1 = 0.2, 0.01
EPS = 1e-5
REC = 6


def flat(ap):
    return ap.rearrange("p a b -> p (a b)")


class Links:

    def __init__(self, eng, sem, start=0):
        self.eng, self.sem, self.n, self.start = eng, sem, 0, start

    def mark(self, ins):
        ins.then_inc(self.sem, 1)
        self.n += 1

    def wait(self):
        self.eng.wait_ge(self.sem, self.start + self.n)

    def link(self, ins):
        self.mark(ins)
        self.wait()


def ticks(eng, groups, ring, depth, f):
    head = -(-(depth + ring) // ring) * ring
    assert groups % ring == 0 and groups > head
    for t in range(head):
        f(t, t % ring, lambda skew: t >= skew)
    with eng.Fori(head // ring, groups // ring) as i:
        for h in range(ring):
            f(i * ring + h, h, lambda skew: True)
    for t in range(groups, groups + depth):
        f(t, t % ring, lambda skew: t - skew < groups)


def pipeline(eng, groups, ring, stages):
    def tick(t, h, has):
        for skew, f in stages:
            if has(skew):
                f(t - skew, (h - skew) % ring)

    ticks(eng, groups, ring, max(skew for skew, _ in stages), tick)


def past(j, n):
    return not isinstance(j, int) or j >= n


def filled(j, slot, ring, inc):
    return (j // ring + 1) * inc if isinstance(j, int) else (j - slot) * (inc // ring) + inc


class Chain:

    def __init__(self, eng, sem, per):
        self.eng, self.sem, self.per, self.n, self.j = eng, sem, per, 0, 0

    def group(self, j):
        assert self.n in (0, self.per), self.n
        self.j, self.n = j, 0

    def mark(self, ins):
        ins.then_inc(self.sem, 1)
        self.n += 1

    def link(self, ins):
        self.mark(ins)
        self.eng.wait_ge(self.sem, self.j * self.per + self.n)


def settle(eng, K):
    eng.sem_inc(K.passed, 1)


def registers(nc, eng, engine, table, k, n, top):
    return nc.values_load_multi_w_load_instructions(table[0:1, ds(k, n)], engines=(engine,), min_val=0, max_val=top)[1]


class Phase:

    def __init__(self, nc, name):
        self.nc, self.name, self.ctx = nc, name, ExitStack()

    def __enter__(self):
        self.ctx.__enter__()
        return self

    def __exit__(self, *e):
        return self.ctx.__exit__(*e)

    def sb(self, name, shape, dt=F32):
        return self.ctx.enter_context(self.nc.sbuf_tensor(f"{self.name}_{name}", shape, dt))

    def ps(self, name, shape):
        n = 1
        for x in shape[1:]:
            n *= x
        t = self.ctx.enter_context(self.nc.psum_tensor(f"{self.name}_{name}", [shape[0], -(-n // 512) * 512], F32))
        if len(shape) == 2:
            return t[:, 0:n]
        dims = dict(zip("bcd", shape[2:]))
        names = " ".join("abcd"[:len(shape) - 1])
        return t[:, 0:n].rearrange(f"p ({names}) -> p {names}", **dims)

    def sem(self, name):
        return self.ctx.enter_context(self.nc.semaphore(f"{self.name}_{name}"))

    def block(self):
        return self.ctx.enter_context(self.nc.Block())


def constants(nc, K):
    with Phase(nc, "const") as ph:
        ramp_i = ph.sb("ramp_i", [P, 256], I32)
        part_i = ph.sb("part_i", [P, 1], I32)
        head_i = ph.sb("head_i", [P, 1], I32)
        grid_i = ph.sb("grid_i", [P, KC], I32)
        headf = ph.sb("headf", [P, 1])
        s_iota, s_v = ph.sem("iota"), ph.sem("v")
        block = ph.block()

        @block.gpsimd
        def _(pool):
            pool.iota(ramp_i[:, :], [[1, 256]], base=0, channel_multiplier=0).then_inc(s_iota, 1)
            pool.iota(part_i[:, :], [[0, 1]], base=0, channel_multiplier=1).then_inc(s_iota, 1)
            pool.iota(grid_i[:, :], [[1, KC]], base=0, channel_multiplier=KC).then_inc(s_iota, 1)

        @block.vector
        def _(dve):
            dve.wait_ge(s_iota, 3)
            L = Links(dve, s_v)
            L.mark(dve.tensor_copy(K.ramp[:, :], ramp_i[:, :]))
            L.mark(dve.tensor_copy(K.part[:, :], part_i[:, :]))
            L.mark(dve.tensor_copy(K.grid[:, :], grid_i[:, :]))
            L.link(dve.tensor_scalar(head_i[:, :], part_i[:, :], 4, None, ALU.arith_shift_right))
            L.link(dve.tensor_copy(headf[:, :], head_i[:, :]))
            L.mark(dve.tensor_scalar(K.ident[:, :], K.ramp[:, 0:P], K.part[:, 0:1], None, ALU.is_equal))
            L.mark(dve.tensor_scalar(K.identb[:, :], K.ramp[:, 0:P], K.part[:, 0:1], None, ALU.is_equal))
            L.mark(dve.tensor_scalar(K.identb128[:, :], K.ramp[:, 0:P], K.part[:, 0:1], float(P), ALU.is_equal, ALU.mult))
            L.mark(dve.tensor_scalar(K.below[:, :], K.ramp[:, 0:P], K.part[:, 0:1], None, ALU.is_lt))
            L.mark(dve.tensor_scalar(K.headmask[:, :], K.ramp[:, 0:H], headf[:, 0:1], None, ALU.is_equal))
            L.mark(dve.tensor_scalar(K.trash[:, :], K.part[:, 0:1], float(NP), None, ALU.add))
            L.link(dve.memset(K.ones[:, :], 1.0))


def schedule(nc, K, T):
    with Phase(nc, "sched") as ph:
        dst = ph.sb("dst", [P, DCOLS], I32)
        win_i = ph.sb("win_i", [P, DCOLS], I32)
        win = ph.sb("win", [P, DCOLS], BF16)
        junk = ph.sb("junk", [P, DCOLS], BF16)
        below = ph.sb("below", [P, WINDOWS + 1])
        off = ph.sb("off", [P, WINDOWS + 1])
        count = ph.sb("count", [P, WINDOWS], I32)
        tiles_i = ph.sb("tiles_i", [P, WINDOWS], I32)
        tiles = ph.sb("tiles", [P, WINDOWS])
        start = ph.sb("start", [P, WINDOWS + 1])
        end = ph.sb("end", [P, WINDOWS])
        shift = ph.sb("shift", [P, WINDOWS + 1])
        cmp = ph.sb("cmp", [P, KC, WINDOWS])
        hot = ph.sb("hot", [P, KC, WINDOWS + 1])
        wk = ph.sb("wk", [P, KC])
        ek = ph.sb("ek", [P, KC])
        w_out = ph.sb("w_out", [P, KC], I32)
        e_out = ph.sb("e_out", [P, KC], I32)
        off_ps = ph.ps("off_ps", [P, WINDOWS + 1])
        s_dst, s_v, s_pe, s_t, s_back = (ph.sem(x) for x in ("dst", "v", "pe", "t", "back"))
        s_cnt = ph.sem("cnt")
        block = ph.block()

        @block.sync
        def _(sp):
            sp.dma_start(dst[:, :], T.dst).then_inc(s_dst, 16)
            sp.wait_ge(s_t, 1)
            sp.dma_start(T.sched_w.rearrange("(p c) -> p c", c=KC), w_out[:, :]).then_inc(s_dst, 16)
            sp.dma_start(T.sched_e.rearrange("(p c) -> p c", c=KC), e_out[:, :]).then_inc(s_dst, 16)
            sp.wait_ge(s_dst, 48)
            settle(sp, K)
            sp.dma_start(K.reg_w[:, :], T.sched_w.rearrange("(a s) -> a s", a=1)).then_inc(s_back, 16)
            sp.dma_start(K.reg_e[:, :], T.sched_e.rearrange("(a s) -> a s", a=1)).then_inc(s_back, 16)
            sp.dma_start(K.wstep_i[:, :], T.sched_w.rearrange("(a s) -> a s", a=1)[:, 0:STEPS]
                         .to_broadcast([P, STEPS])).then_inc(s_back, 16)
            sp.wait_ge(s_back, 48)

        @block.tensor
        def _(pe):
            pe.wait_ge(s_cnt, WINDOWS + 1)
            pe.matmul(off_ps[:, :], K.ones[:, :], below[:, :], start=True, stop=True).then_inc(s_pe, 1)

        @block.vector
        def _(dve):
            L = Links(dve, s_v)
            dve.wait_ge(s_dst, 16)
            L.link(dve.tensor_scalar(win_i[:, :], dst[:, :], 6, None, ALU.arith_shift_right))
            L.link(dve.tensor_copy(win[:, :], win_i[:, :]))
            with dve.Fori(0, WINDOWS + 1) as w:
                dve.tensor_scalar(junk[:, :], win[:, :], K.ramp[:, ds(w, 1)], 0.0, ALU.is_lt, ALU.add,
                                  accum_out=below[:, ds(w, 1)]).then_inc(s_cnt, 1)
                dve.wait_ge(s_cnt, w + 1)
            dve.wait_ge(s_pe, 1)
            L.link(dve.tensor_copy(off[:, :], off_ps[:, :]))
            W = WINDOWS
            L.link(dve.tensor_tensor(count[:, :], off[:, 1:W + 1], off[:, 0:W], ALU.subtract))
            L.link(dve.tensor_scalar(count[:, :], count[:, :], float(P - 1), None, ALU.add))
            L.link(dve.tensor_scalar(tiles_i[:, :], count[:, :], 7, None, ALU.arith_shift_right))
            L.link(dve.tensor_copy(tiles[:, :], tiles_i[:, :]))
            L.link(dve.tensor_tensor_scan(end[:, :], K.ones[:, 0:W], tiles[:, :], 0.0, ALU.mult, ALU.add))
            L.mark(dve.tensor_tensor(start[:, 0:W], end[:, :], tiles[:, :], ALU.subtract))
            L.link(dve.tensor_copy(start[:, W:W + 1], end[:, W - 1:W]))
            L.link(dve.scalar_tensor_tensor(shift[:, :], start[:, :], -float(P), off[:, :], ALU.mult, ALU.add))
            L.link(dve.tensor_tensor(cmp[:, :, :], end[:, :].unsqueeze(1).to_broadcast([P, KC, W]),
                                     K.grid[:, :].unsqueeze(2).to_broadcast([P, KC, W]), ALU.is_le))
            L.link(dve.tensor_reduce(wk[:, :], cmp[:, :, :], AX.X, ALU.add))
            L.link(dve.tensor_tensor(hot[:, :, :], K.ramp[:, 0:W + 1].unsqueeze(1).to_broadcast([P, KC, W + 1]),
                                     wk[:, :].unsqueeze(2).to_broadcast([P, KC, W + 1]), ALU.is_equal))
            L.link(dve.tensor_tensor(hot[:, :, :], hot[:, :, :],
                                     shift[:, :].unsqueeze(1).to_broadcast([P, KC, W + 1]), ALU.mult))
            L.link(dve.tensor_reduce(ek[:, :], hot[:, :, :], AX.X, ALU.add))
            L.link(dve.scalar_tensor_tensor(ek[:, :], K.grid[:, :], float(P), ek[:, :], ALU.mult, ALU.add))
            L.link(dve.tensor_scalar(e_out[:, :], ek[:, :], float(N_EDGES), None, ALU.min))
            dve.tensor_scalar(w_out[:, :], wk[:, :], float(W - 1), None, ALU.min).then_inc(s_t, 1)
            dve.wait_ge(s_back, 48)
            L.link(dve.tensor_scalar(K.wbase[:, :], K.wstep_i[:, :], float(WIN), None, ALU.mult))



def node_inputs(nc, K, T):
    with Phase(nc, "node") as ph:
        NA = 2 * R + 2
        YW = R * H + C + 2 * H
        x = ph.sb("x", [P, TILES, C])
        stats = ph.sb("stats", [P, 2, 6])
        mv = ph.sb("mv", [P, 2, 2])
        mean = ph.sb("mean", [P, TILES])
        rstd = ph.sb("rstd", [P, TILES])
        nmr = ph.sb("nmr", [P, TILES])
        w_rel = ph.sb("w_rel", [P, R, C])
        w_y = ph.sb("w_y", [P, YW])
        w_ed = ph.sb("w_ed", [P, R, H])
        w_t = ph.sb("w_t", [P, R + 1, C])
        att = ph.sb("att", [P, NA])
        adiag = ph.sb("adiag", [P, NA, H])
        h = ph.sb("h", [P, 2, C])
        hT = ph.sb("hT", [P, 2, P])
        rows = ph.sb("rows", [P, 2, R, XR])
        srow = ph.sb("srow", [P, 2, C + 2 * H])
        hT_ps = [ph.ps(f"hT_ps{b}", [P, P]) for b in range(2)]
        x_ps = [ph.ps(f"x_ps{b}", [P, R, C]) for b in range(2)]
        y_ps = [ph.ps(f"y_ps{b}", [P, YW]) for b in range(2)]
        e_ps = [ph.ps(f"e_ps{b}", [WIN, 2, R * H]) for b in range(2)]
        s_w, s_x, s_v, s_adiag, s_fold, s_stat, s_var, s_sd, s_norm = (
            ph.sem(n) for n in ("w", "x", "v", "adiag", "fold", "stat", "var", "sd", "norm"))
        s_h, s_hT, s_hTs, s_prod, s_rel, s_small = (ph.sem(n) for n in ("h", "hT", "hTs", "prod", "rel", "small"))
        s_st = [ph.sem(f"st{b}") for b in range(2)]
        block = ph.block()

        @block.sync
        def _(sp):
            sp.dma_start(x[:, :, :], T.x.rearrange("(t p) c -> p t c", p=P)).then_inc(s_x, 16)
            sp.dma_start(w_rel[:, :, :], T.W_rel.rearrange("r i o -> i r o")).then_inc(s_w, 16)
            sp.dma_start(w_y[:, R * H:R * H + C], T.W_self).then_inc(s_w, 16)
            sp.dma_start(w_t[:, 0:R, :], T.W_relT.rearrange("r o i -> o r i")).then_inc(s_w, 16)
            sp.dma_start(w_t[:, R, :], T.W_selfT).then_inc(s_w, 16)
            sp.dma_start(att[:, :], T.att).then_inc(s_w, 16)

            def store(t, b):
                sp.wait_ge(s_rel, t + 1)
                sp.wait_ge(s_small, t + 1)
                sp.dma_start(T.xrel.rearrange("(r n) c -> n r c", r=R)[ds(t * P, P), :, :],
                             rows[:, b, :, :]).then_inc(s_st[b], 16)
                sp.dma_start(T.esrc.rearrange("(r n) c -> n r c", r=R)[ds(t * P, P), :, :],
                             rows[:, b, :, C:XR]).then_inc(s_st[b], 16)
                sp.dma_start(T.srow[ds(t * P, P), :], srow[:, b, :]).then_inc(s_st[b], 16)

            pipeline(sp, TILES, 2, [(0, store)])
            for b in range(2):
                sp.wait_ge(s_st[b], 48 * (TILES // 2))

        @block.vector
        def _(dve):
            L = Links(dve, s_v)
            dve.wait_ge(s_w, 80)
            dve.tensor_tensor(adiag[:, :, :], att[:, :].unsqueeze(2).to_broadcast([P, NA, H]),
                              K.headmask[:, :].unsqueeze(1).to_broadcast([P, NA, H]), ALU.mult).then_inc(s_adiag, 1)
            dve.wait_ge(s_fold, 1)
            f = x_ps[0][:, 0, 0:2 * R * H].rearrange("p (r s h) -> p r s h", r=R, s=2)
            L.mark(dve.tensor_copy(w_y[:, 0:R * H].rearrange("p (r h) -> p r h", r=R), f[:, :, 0, :]))
            L.mark(dve.tensor_copy(w_ed[:, :, :], f[:, :, 1, :]))
            L.mark(dve.tensor_copy(w_y[:, R * H + C:YW], y_ps[0][:, 0:2 * H]))
            dve.wait_ge(s_x, 16)
            chain = Chain(dve, s_stat, 4)

            def statistics(t, b):
                chain.group(t)
                chain.link(dve.bn_stats(stats[:, b, :], x[:, ds(t, 1), :].rearrange("p a c -> p (a c)")))
                settle(dve, K)
                chain.link(dve.bn_aggr(mv[:, b, :], stats[:, b, :]))
                chain.mark(dve.tensor_copy(mean[:, ds(t, 1)], mv[:, b, 0:1]))
                chain.mark(dve.tensor_scalar(rstd[:, ds(t, 1)], mv[:, b, 1:2], EPS, None, ALU.add))

            pipeline(dve, TILES, 2, [(0, statistics)])
            dve.wait_ge(s_stat, 4 * TILES)
            dve.sem_inc(s_var, 1)
            dve.wait_ge(s_sd, 1)
            L.link(dve.reciprocal(rstd[:, :], rstd[:, :]))
            dve.scalar_tensor_tensor(nmr[:, :], mean[:, :], -1.0, rstd[:, :], ALU.mult, ALU.mult).then_inc(s_norm, 1)

            def evacuate(t, b):
                dve.wait_ge(s_hT, t + 1)
                if past(t, 2):
                    dve.wait_ge(s_prod, t - 1)
                dve.tensor_copy(hT[:, b, :], hT_ps[b][:, :]).then_inc(s_hTs, 1)
                dve.wait_ge(s_prod, t + 1)
                if past(t, 2):
                    dve.wait_ge(s_st[b], (t - b) * 24)
                dve.tensor_copy(rows[:, b, :, C:XR], y_ps[b][:, 0:R * H].rearrange("p (r h) -> p r h", r=R))
                dve.tensor_copy(srow[:, b, :], y_ps[b][:, R * H:YW])
                dve.tensor_copy(K.ed[:, ds(t * 2, 2), :], e_ps[b][:, :, :]).then_inc(s_small, 1)

            pipeline(dve, TILES, 2, [(0, evacuate)])

        @block.scalar
        def _(act):
            act.wait_ge(s_var, 1)
            act.activation(rstd[:, :], rstd[:, :], ACT.Sqrt).then_inc(s_sd, 1)
            act.wait_ge(s_norm, 1)

            def normalize(t, b):
                if past(t, 2):
                    act.wait_ge(s_hT, t - 1)
                act.activation(h[:, b, :], x[:, ds(t, 1), :].rearrange("p a c -> p (a c)"), ACT.Relu,
                               bias=nmr[:, ds(t, 1)], scale=rstd[:, ds(t, 1)]).then_inc(s_h, 1)

            def evacuate(t, b):
                act.wait_ge(s_prod, t + 1)
                if past(t, 2):
                    act.wait_ge(s_st[b], (t - b) * 24)
                act.activation(rows[:, b, :, 0:C], x_ps[b][:, :, :], ACT.Copy).then_inc(s_rel, 1)

            pipeline(act, TILES, 2, [(0, normalize), (1, evacuate)])

        @block.tensor
        def _(pe):
            pe.wait_ge(s_w, 80)
            pe.wait_ge(s_adiag, 1)
            for r in range(R):
                pe.matmul(x_ps[0][:, 0, r * 2 * H:(r + 1) * 2 * H], w_t[:, r, :],
                          flat(adiag[:, 2 * r:2 * r + 2, :]), start=True, stop=True)
            pe.matmul(y_ps[0][:, 0:2 * H], w_t[:, R, :], flat(adiag[:, 2 * R:NA, :]),
                      start=True, stop=True).then_inc(s_fold, 1)
            pe.wait_ge(s_v, 3)

            def transpose(t, b):
                pe.wait_ge(s_h, t + 1)
                if past(t, 2):
                    pe.wait_ge(s_hTs, t - 1)
                pe.transpose(hT_ps[b][:, :], h[:, b, :], K.ident[:, :]).then_inc(s_hT, 1)

            def products(t, b):
                pe.wait_ge(s_hTs, t + 1)
                if past(t, 2):
                    pe.wait_ge(s_rel, t - 1)
                    pe.wait_ge(s_small, t - 1)
                pe.matmul(flat(x_ps[b][:, :, :]), hT[:, b, :], flat(w_rel[:, :, :]), start=True, stop=True)
                pe.matmul(y_ps[b][:, :], hT[:, b, :], w_y[:, :], start=True, stop=True)
                for q in range(2):
                    last = pe.matmul(e_ps[b][:, q, :], hT[:, b, q * WIN:(q + 1) * WIN], flat(w_ed[:, :, :]),
                                     start=True, stop=True)
                last.then_inc(s_prod, 1)

            pipeline(pe, TILES, 2, [(0, transpose), (0, products)])


def relation_maxima(nc, K, T):
    with Phase(nc, "max") as ph:
        GROUPS = STEPS // G
        rec = ph.sb("rec", [P, 2, G, REC], I32)
        idx = ph.sb("idx", [P, 2, G], I32)
        isnext = ph.sb("isnext", [P, 2, G])
        isprev = ph.sb("isprev", [P, 2, G])
        lastloc = ph.sb("lastloc", [P, 2, G])
        begins = ph.sb("begins", [P, STEPS], BF16)
        mask = ph.sb("mask", [P, 2, G, R])
        outside = ph.sb("outside", [P, 2, G, R])
        es = ph.sb("es", [P, 2, G, H])
        beg = ph.sb("beg", [P, 2, G], BF16)
        m = ph.sb("m", [P, 2, G, R * H])
        mT = ph.sb("mT", [R * H, 2, G * P])
        run = ph.sb("run", [R * H, 2, G * P])
        runT = ph.sb("runT", [P, 2, G, R * H + 1])
        onehot = ph.sb("onehot", [P, 2, G, WIN])
        maxima = ph.sb("maxima", [WIN, WSLOTS, R * H + 1])
        mm = ph.sb("mm", [WIN, WSLOTS, R, H])
        both = ph.sb("both", [WIN, WSLOTS, R, 2, H])
        valid = ph.sb("valid", [WIN, WSLOTS, R])
        none = ph.sb("none", [WIN, WSLOTS])
        mT_ps = ph.ps("mT_ps", [R * H, G * P])
        beg_ps = ph.ps("beg_ps", [R * H, G * P])
        runT_ps = ph.ps("runT_ps", [P, G, R * H])
        node_ps = [ph.ps(f"node_ps{b}", [WIN, G, R * H + 1]) for b in range(2)]
        s_rec = [ph.sem(f"rec{b}") for b in range(2)]
        s_es = [ph.sem(f"es{b}") for b in range(2)]
        s_pc, s_prep, s_mc, s_m, s_tr, s_mt, s_scan, s_bk, s_rt, s_oh, s_node, s_acc = (
            ph.sem(n) for n in ("pc", "prep", "mc", "m", "tr", "mt", "scan", "bk", "rt", "oh", "node", "acc"))
        s_init, s_end, s_fin, s_out = (ph.sem(n) for n in ("init", "end", "fin", "out"))
        block = ph.block()

        @block.sync
        def _(sp):
            def load(j, b):
                e = registers(nc, sp, mybir.EngineType.SP, K.reg_e, j * G, G, N_EDGES)
                if past(j, 2):
                    sp.wait_ge(s_prep, j - 1)
                for u in range(G):
                    sp.dma_start(rec[:, b, u, :], T.rec[ds(e[u], P), :]).then_inc(s_rec[b], 16)

            pipeline(sp, GROUPS, 2, [(0, load)])
            sp.wait_ge(s_fin, 1)
            sp.dma_start(T.edm.rearrange("(w n) c -> n w c", n=WIN),
                         both[:, :, :, :, :].rearrange("n w r s h -> n w (r s h)")).then_inc(s_out, 16)
            sp.dma_start(T.valid.rearrange("(w n) r -> n w r", n=WIN), valid[:, :, :]).then_inc(s_out, 16)
            sp.wait_ge(s_out, 32)

        @block.gpsimd
        def _(pool):
            def gather(j, b):
                pool.wait_ge(s_prep, j + 1)
                if past(j, 2):
                    pool.wait_ge(s_m, j - 1)
                settle(pool, K)
                for u in range(G):
                    pool.indirect_dma_start(es[:, b, u, :], None, T.esrc,
                                            bass.IndirectOffsetOnAxis(ap=idx[:, b, u:u + 1], axis=0)).then_inc(s_es[b], 16)

            pipeline(pool, GROUPS, 2, [(0, gather)])

        @block.vector
        def _(dve):
            dve.memset(maxima[:, :, :], 0.0).then_inc(s_init, 1)
            dve.memset(runT[:, :, :, R * H:], 1.0).then_inc(s_init, 1)
            dve.wait_ge(s_init, 2)
            pc, mc = Chain(dve, s_pc, 12), Chain(dve, s_mc, 2)
            rel4 = K.ramp[:, 0:R].unsqueeze(1).to_broadcast([P, G, R])

            def prepare(j, b):
                k = j * G
                src, dst, typ, prev, nxt = (rec[:, b, :, c] for c in range(5))
                dve.wait_ge(s_rec[b], filled(j, b, 2, 16 * G))
                pc.group(j)
                loc, key = K.loc[:, ds(k, G)], K.key[:, ds(k, G)]
                pc.mark(dve.tensor_tensor(isnext[:, b, :], dst, nxt, ALU.not_equal))
                pc.mark(dve.tensor_tensor(isprev[:, b, :], dst, prev, ALU.not_equal))
                pc.mark(dve.tensor_tensor(loc, dst, K.wbase[:, ds(k, G)], ALU.subtract))
                pc.mark(dve.tensor_tensor(mask[:, b, :, :], rel4, typ.unsqueeze(2).to_broadcast([P, G, R]), ALU.is_equal))
                pc.mark(dve.scalar_tensor_tensor(idx[:, b, :], typ, float(NP), src, ALU.mult, ALU.add))
                pc.mark(dve.scalar_tensor_tensor(K.idx[:, ds(k, G)], typ, float(NP), src, ALU.mult, ALU.add))
                pc.mark(dve.tensor_copy(K.src[:, ds(k, G)], src))
                pc.link(dve.tensor_copy(K.typ[:, ds(k, G)], typ))
                pc.mark(dve.scalar_tensor_tensor(key, loc, float(R), typ, ALU.mult, ALU.add))
                pc.mark(dve.tensor_scalar(outside[:, b, :, :], mask[:, b, :, :], 1.0, BIG, ALU.subtract, ALU.mult))
                pc.mark(dve.tensor_scalar(begins[:, ds(k, G)], isprev[:, b, :], -BIG, None, ALU.mult))
                pc.link(dve.scalar_tensor_tensor(lastloc[:, b, :], loc, 1.0, isnext[:, b, :], ALU.add, ALU.mult))
                dve.tensor_scalar(lastloc[:, b, :], lastloc[:, b, :], 1.0, None, ALU.subtract).then_inc(s_prep, 1)

            def separate(j, b):
                dve.wait_ge(s_es[b], filled(j, b, 2, 16 * G))
                dve.wait_ge(s_prep, j + 1)
                if past(j, 2):
                    dve.wait_ge(s_tr, j - 1)
                mc.group(j)
                m4 = m[:, b, :, :].rearrange("p g (r h) -> p g r h", r=R)
                mc.mark(dve.tensor_tensor(m4, es[:, b, :, :].unsqueeze(2).to_broadcast([P, G, R, H]),
                                          mask[:, b, :, :].unsqueeze(3).to_broadcast([P, G, R, H]), ALU.mult))
                mc.link(dve.tensor_copy(beg[:, b, :], begins[:, ds(j * G, G)]))
                dve.tensor_tensor(m4, m4, outside[:, b, :, :].unsqueeze(3).to_broadcast([P, G, R, H]), ALU.add).then_inc(s_m, 1)
                if past(j, 2):
                    dve.wait_ge(s_node, j - 1)
                dve.tensor_tensor(onehot[:, b, :, :], K.ramp[:, 0:WIN].unsqueeze(1).to_broadcast([P, G, WIN]),
                                  lastloc[:, b, :].unsqueeze(2).to_broadcast([P, G, WIN]), ALU.is_equal).then_inc(s_oh, 1)

            def scan(j, b):
                dve.wait_ge(s_mt, j + 1)
                if past(j, 1):
                    dve.wait_ge(s_scan, j)
                if past(j, 2):
                    dve.wait_ge(s_bk, j - 1)
                first = isinstance(j, int) and j == 0
                dve.tensor_tensor_scan(run[:, b, :], beg_ps[:, :], mT[:, b, :],
                                       -BIG if first else run[:, 1 - b, G * P - 1:G * P],
                                       ALU.add, ALU.max).then_inc(s_scan, 1)

            def keep(j, b):
                dve.wait_ge(s_node, j + 1)
                w = registers(nc, dve, mybir.EngineType.DVE, K.reg_w, j * G, G, WINDOWS - 1)
                for u in range(G):
                    if u or past(j, 1):
                        dve.wait_ge(s_acc, j * G + u)
                    dst = maxima[:, ds(w[u], 1), :].rearrange("n a c -> n (a c)")
                    dve.tensor_tensor(dst, dst, node_ps[b][:, u, :], ALU.add).then_inc(s_acc, 1)

            pipeline(dve, GROUPS, 2, [(4, keep), (3, scan), (2, separate), (0, prepare)])
            L = Links(dve, s_end)
            dve.wait_ge(s_acc, STEPS)
            ed4 = K.ed[:, :, :].rearrange("n w (r h) -> n w r h", r=R)
            mx = maxima[:, :, 0:R * H].rearrange("n w (r h) -> n w r h", r=R)
            wr = "n w r h -> n (w r) h"
            L.link(dve.tensor_scalar(none[:, :], maxima[:, :, R * H], 1.0, BIG, ALU.subtract, ALU.mult))
            L.link(dve.tensor_tensor(mm[:, :, :, :], mx, none[:, :].unsqueeze(2).unsqueeze(3)
                                     .to_broadcast([WIN, WSLOTS, R, H]), ALU.add))
            L.link(dve.tensor_scalar(valid[:, :, :], mm[:, :, :, 0], -0.9 * BIG, None, ALU.is_gt))
            L.link(dve.tensor_tensor(mm[:, :, :, :], mm[:, :, :, :], ed4, ALU.add))
            bv = both[:, :, :, :, :].rearrange("n w r s h -> n (w r) s h")
            L.mark(dve.scalar_tensor_tensor(bv[:, :, 1, :], mm[:, :, :, :].rearrange(wr), SLOPE0,
                                            mm[:, :, :, :].rearrange(wr), ALU.mult, ALU.max))
            L.link(dve.tensor_copy(bv[:, :, 0, :], ed4.rearrange(wr)))
            dve.sem_inc(s_fin, 1)

        @block.scalar
        def _(act):
            def move(j, b):
                act.wait_ge(s_tr, j + 1)
                if past(j, 2):
                    act.wait_ge(s_scan, j - 1)
                act.activation(mT[:, b, :], mT_ps[:, :], ACT.Copy).then_inc(s_mt, 1)

            def move_back(j, b):
                act.wait_ge(s_bk, j + 1)
                if past(j, 2):
                    act.wait_ge(s_node, j - 1)
                act.activation(runT[:, b, :, 0:R * H], runT_ps[:, :, :], ACT.Copy).then_inc(s_rt, 1)

            act.wait_ge(s_init, 2)
            pipeline(act, GROUPS, 2, [(1, move_back), (0, move)])

        @block.tensor
        def _(pe):
            def transpose(j, b):
                pe.wait_ge(s_m, j + 1)
                if past(j, 1):
                    pe.wait_ge(s_mt, j)
                    pe.wait_ge(s_scan, j)
                settle(pe, K)
                for u in range(G):
                    pe.transpose(mT_ps[:, u * P:(u + 1) * P], m[:, b, u, :], K.ident[:, :])
                for u in range(G):
                    last = pe.matmul(beg_ps[:, u * P:(u + 1) * P], beg[:, b, u:u + 1].to_broadcast([P, R * H]),
                                     K.identb[:, :], start=True, stop=True)
                last.then_inc(s_tr, 1)

            def back(j, b):
                pe.wait_ge(s_scan, j + 1)
                if past(j, 1):
                    pe.wait_ge(s_rt, j)
                settle(pe, K)
                for u in range(G):
                    last = pe.transpose(runT_ps[:, u, :], run[:, b, u * P:(u + 1) * P], K.ident[0:R * H, 0:R * H])
                last.then_inc(s_bk, 1)

            def by_node(j, b):
                pe.wait_ge(s_rt, j + 1)
                pe.wait_ge(s_oh, j + 1)
                if past(j, 2):
                    pe.wait_ge(s_acc, (j - 1) * G)
                for u in range(G):
                    last = pe.matmul(node_ps[b][:, u, :], onehot[:, b, u, :], runT[:, b, u, :], start=True, stop=True)
                last.then_inc(s_node, 1)

            pe.wait_ge(s_init, 2)
            pipeline(pe, GROUPS, 2, [(2, by_node), (1, back), (0, transpose)])


def relation_attention(nc, K, T, acc):
    with Phase(nc, "att") as ph:
        U, RG = 4, 4
        GROUPS = STEPS // U
        S2 = 2 * H
        idx = ph.sb("idx", [P, RG, U], I32)
        xg = ph.sb("xg", [P, RG, U, XR])
        onehot = ph.sb("onehot", [P, RG, U, WIN])
        onehotT = ph.sb("onehotT", [WIN, RG, U * P])
        edw = ph.sb("edw", [WIN, RG, U, R * S2])
        mask = ph.sb("mask", [P, RG, U, R])
        masked = ph.sb("masked", [P, U, R, S2])
        dstv = ph.sb("dstv", [P, U, S2])
        logit = ph.sb("logit", [P, U, H])
        leaky = ph.sb("leaky", [P, U, H])
        arg = ph.sb("arg", [P, RG, U, H])
        p = ph.sb("p", [P, RG, U, H])
        px = ph.sb("px", [P, RG, U, XR])
        keyhot = ph.sb("keyhot", [P, 2, U, R * WIN])
        oT_ps = [ph.ps(f"oT_ps{b}", [WIN, U * P]) for b in range(1)]
        dst_ps = [ph.ps(f"dst_ps{b}", [P, U, R * S2]) for b in range(2)]
        sum_ps = [ph.ps(f"sum_ps{u}", [P, 2, XR]) for u in range(U)]
        s_xg = [ph.sem(f"xg{b}") for b in range(RG)]
        s_ed = [ph.sem(f"ed{b}") for b in range(RG)]
        s_idx, s_oh, s_tr, s_oT, s_dst, s_sc, s_sel, s_p, s_pc, s_px, s_kh, s_sum, s_acc = (
            ph.sem(n) for n in ("idx", "oh", "tr", "oT", "dst", "sc", "sel", "p", "pc", "px", "kh", "sum", "acc"))
        block = ph.block()

        @block.sync
        def _(sp):
            def load(j, b):
                w = registers(nc, sp, mybir.EngineType.SP, K.reg_w, j * U, U, WINDOWS - 1)
                if past(j, RG):
                    sp.wait_ge(s_dst, j - RG + 1)
                    settle(sp, K)
                for u in range(U):
                    sp.dma_start(edw[:, b, u, :], T.edm[ds(w[u] * WIN, WIN), :]).then_inc(s_ed[b], 16)

            pipeline(sp, GROUPS, RG, [(0, load)])

        @block.gpsimd
        def _(pool):
            def gather(j, b):
                pool.wait_ge(s_idx, j + 1)
                if past(j, RG):
                    pool.wait_ge(s_px, j - RG + 1)
                settle(pool, K)
                for u in range(U):
                    pool.indirect_dma_start(xg[:, b, u, :], None, T.xrel,
                                            bass.IndirectOffsetOnAxis(ap=idx[:, b, u:u + 1], axis=0)).then_inc(s_xg[b], 16)

            pipeline(pool, GROUPS, RG, [(0, gather)])

        @block.vector
        def _(dve):
            dve.memset(acc[:, :, :, :], 0.0).then_inc(s_acc, 1)
            dve.wait_ge(s_acc, 1)

            def indices(j, b):
                dve.tensor_copy(idx[:, b, :], K.idx[:, ds(j * U, U)]).then_inc(s_idx, 1)

            def hots(j, b):
                if past(j, RG):
                    dve.wait_ge(s_tr, j - RG + 1)
                dve.tensor_tensor(mask[:, b, :, :], K.ramp[:, 0:R].unsqueeze(1).to_broadcast([P, U, R]),
                                  K.typ[:, ds(j * U, U)].unsqueeze(2).to_broadcast([P, U, R]), ALU.is_equal)
                dve.tensor_tensor(onehot[:, b, :, :], K.ramp[:, 0:WIN].unsqueeze(1).to_broadcast([P, U, WIN]),
                                  K.loc[:, ds(j * U, U)].unsqueeze(2).to_broadcast([P, U, WIN]), ALU.is_equal).then_inc(s_oh, 1)

            def keyhots(j, b, u):
                if past(j, 2) and u == 0:
                    dve.wait_ge(s_sum, (j - 1) * U)
                dve.tensor_scalar(keyhot[:, b % 2, u, :], K.ramp[:, :], K.key[:, ds(j * U + u, 1)], None,
                                  ALU.is_equal).then_inc(s_kh, 1)

            def select(j, b, step):
                if step == 0:
                    dve.wait_ge(s_dst, j + 1)
                    dve.wait_ge(s_oh, j + 1)
                    ins = dve.tensor_tensor(masked[:, :, :, :], dst_ps[b % 2][:, :, :].rearrange("p u (r c) -> p u r c", r=R),
                                            mask[:, b, :, :].unsqueeze(3).to_broadcast([P, U, R, S2]), ALU.mult)
                    ins.then_inc(s_sc, 1)
                    return
                dve.wait_ge(s_sc, j * 4 + step)
                if step == 1:
                    ins = dve.tensor_reduce(dstv[:, :, :], masked[:, :, :, :].rearrange("p u r c -> p u c r"), AX.X, ALU.add)
                elif step == 2:
                    dve.wait_ge(s_xg[b], filled(j, b, RG, 16 * U))
                    ins = dve.tensor_tensor(logit[:, :, :], xg[:, b, :, C:XR], dstv[:, :, 0:H], ALU.add)
                elif step == 3:
                    ins = dve.scalar_tensor_tensor(leaky[:, :, :], logit[:, :, :], SLOPE0, logit[:, :, :], ALU.mult, ALU.max)
                else:
                    if past(j, RG):
                        dve.wait_ge(s_p, j - RG + 1)
                    dve.tensor_tensor(arg[:, b, :, :], leaky[:, :, :], dstv[:, :, H:S2], ALU.subtract).then_inc(s_sel, 1)
                    return
                ins.then_inc(s_sc, 1)

            def bound(j, b):
                dve.wait_ge(s_p, j + 1)
                if past(j, RG):
                    dve.wait_ge(s_sum, (j - RG + 1) * U)
                dve.tensor_scalar(px[:, b, :, C:XR], p[:, b, :, :], 1.0, None, ALU.min).then_inc(s_pc, 1)

            def weigh(j, b):
                dve.wait_ge(s_pc, j + 1)
                dve.tensor_tensor(px[:, b, :, 0:C].rearrange("p u (h d) -> p u h d", h=H),
                                  xg[:, b, :, 0:C].rearrange("p u (h d) -> p u h d", h=H),
                                  px[:, b, :, C:XR].unsqueeze(3).to_broadcast([P, U, H, D]), ALU.mult).then_inc(s_px, 1)

            def add(j, b, u, w):
                dve.wait_ge(s_sum, j * U + u + 1)
                dve.wait_ge(s_acc, j * U + u + 1)
                dst = acc[:, ds(w, 1), :, :].rearrange("n a b c -> n (a b c)")
                dve.tensor_tensor(dst, dst, flat(sum_ps[u][:, :, :]), ALU.add).then_inc(s_acc, 1)

            def tick(t, h, has):
                slot = lambda skew: (h - skew) % RG
                if has(5):
                    w = registers(nc, dve, mybir.EngineType.DVE, K.reg_w, (t - 5) * U, U, WINDOWS - 1)
                if has(4):
                    bound(t - 4, slot(4))
                if has(0):
                    indices(t, h)
                if has(3):
                    select(t - 3, slot(3), 0)
                if has(4):
                    weigh(t - 4, slot(4))
                for u in range(U):
                    if has(5):
                        add(t - 5, slot(5), u, w[u])
                    if has(3):
                        select(t - 3, slot(3), u + 1)
                        keyhots(t - 3, slot(3), u)
                if has(1):
                    hots(t - 1, slot(1))

            ticks(dve, GROUPS, RG, 5, tick)
            dve.wait_ge(s_acc, STEPS + 1)

        @block.scalar
        def _(act):
            def move(j, b):
                act.wait_ge(s_tr, j + 1)
                if past(j, RG):
                    act.wait_ge(s_dst, j - RG + 1)
                act.activation(onehotT[:, b, :], oT_ps[0][:, :], ACT.Copy).then_inc(s_oT, 1)

            def exponentials(j, b):
                act.wait_ge(s_sel, j + 1)
                if past(j, RG):
                    act.wait_ge(s_px, j - RG + 1)
                act.activation(p[:, b, :, :], arg[:, b, :, :], ACT.Exp).then_inc(s_p, 1)

            pipeline(act, GROUPS, RG, [(1, exponentials), (0, move)])

        @block.tensor
        def _(pe):
            def transpose(j, b):
                pe.wait_ge(s_oh, j + 1)
                if past(j, 1):
                    pe.wait_ge(s_oT, j)
                settle(pe, K)
                for u in range(U):
                    last = pe.transpose(oT_ps[0][:, u * P:(u + 1) * P], onehot[:, b, u, :], K.ident[:, :])
                last.then_inc(s_tr, 1)

            def expand(j, b):
                pe.wait_ge(s_oT, j + 1)
                pe.wait_ge(s_ed[b], filled(j, b, RG, 16 * U))
                if past(j, 2):
                    pe.wait_ge(s_sel, j - 1)
                for u in range(U):
                    last = pe.matmul(dst_ps[b % 2][:, u, :], onehotT[:, b, u * P:(u + 1) * P], edw[:, b, u, :],
                                     start=True, stop=True)
                last.then_inc(s_dst, 1)

            def sums(j, b):
                pe.wait_ge(s_kh, (j + 1) * U)
                pe.wait_ge(s_px, j + 1)
                for u in range(U):
                    if past(j, 1):
                        pe.wait_ge(s_acc, (j - 1) * U + u + 2)
                    for q in range(2):
                        last = pe.matmul(sum_ps[u][:, q, :], keyhot[:, b % 2, u, q * P:(q + 1) * P], px[:, b, u, :],
                                         start=True, stop=True)
                    last.then_inc(s_sum, 1)

            pipeline(pe, GROUPS, RG, [(3, sums), (0, transpose), (1, expand)])


def node_update(nc, K, T, acc):
    with Phase(nc, "upd") as ph:
        CH = 4
        HALVES = WSLOTS * 2
        acc_h = acc[:, :, :, :].rearrange("p w q c -> p (w q) c")
        bias = ph.sb("bias", [P, C])
        rden = ph.sb("rden", [P, 2, CH, H])
        tmp = ph.sb("tmp", [P, 2, CH, C])
        s_b, s_c, s_g, s_gd = (ph.sem(n) for n in ("b", "c", "g", "gd"))
        block = ph.block()

        @block.sync
        def _(sp):
            sp.dma_start(bias[:, :], T.bias_rel.unsqueeze(0).to_broadcast([P // R, R, C])).then_inc(s_b, 16)
            sp.wait_ge(s_b, 16)

        @block.vector
        def _(dve):
            c = Chain(dve, s_c, 3)
            dve.wait_ge(s_b, 16)

            def normalize(j, b):
                c.group(j)
                if past(j, 2):
                    dve.wait_ge(s_gd, j - 1)
                part = acc_h[:, ds(j * CH, CH), :]
                c.link(dve.tensor_scalar(rden[:, b, :, :], part[:, :, C:XR], 1e-30, None, ALU.max))
                c.link(dve.reciprocal(rden[:, b, :, :], rden[:, b, :, :]))
                c.link(dve.tensor_tensor(tmp[:, b, :, :].rearrange("p k (h d) -> p k h d", h=H),
                                         part[:, :, 0:C].rearrange("p k (h d) -> p k h d", h=H),
                                         rden[:, b, :, :].unsqueeze(3).to_broadcast([P, CH, H, D]), ALU.mult))
                dve.tensor_tensor(tmp[:, b, :, :], tmp[:, b, :, :],
                                  bias[:, :].unsqueeze(1).to_broadcast([P, CH, C]), ALU.add).then_inc(s_g, 1)

            pipeline(dve, HALVES // CH, 2, [(0, normalize)])

        @block.scalar
        def _(act):
            def gelu(j, b):
                act.wait_ge(s_g, j + 1)
                act.activation(acc_h[:, ds(j * CH, CH), 0:C], tmp[:, b, :, :], ACT.Gelu).then_inc(s_gd, 1)

            pipeline(act, HALVES // CH, 2, [(0, gelu)])
            act.wait_ge(s_gd, HALVES // CH)

    with Phase(nc, "mix") as ph:
        M = R + 1
        CR = C + H
        x = ph.sb("x", [P, 2, C])
        srow = ph.sb("srow", [P, 2, C + 2 * H])
        w_c = ph.sb("w_c", [P, CR])
        w_cT = ph.sb("w_cT", [P, C])
        att = ph.sb("att", [P, 2 * R + 2])
        adiag = ph.sb("adiag", [P, H])
        blang = ph.sb("blang", [P, C])
        valid = ph.sb("valid", [P, TILES, R])
        hide = ph.sb("hide", [P, TILES, R])
        g = ph.sb("g", [P, 2, 4, C])
        gT = ph.sb("gT", [P, 2, 4 * P])
        ent = ph.sb("ent", [P, 2, M, C])
        ls = ph.sb("ls", [P, 2, M, H])
        t1 = ph.sb("t1", [P, M, H])
        top = ph.sb("top", [P, H])
        al = ph.sb("al", [P, 2, M, H])
        ex = ph.sb("ex", [P, 2, M, H])
        den = ph.sb("den", [P, H])
        prod = ph.sb("prod", [P, M, C])
        out = ph.sb("out", [P, 2, C])
        zero = ph.sb("zero", [P, 4 * HID])
        gT_ps = [ph.ps(f"gT_ps{b}", [P, 4 * P]) for b in range(2)]
        h_ps = [[ph.ps(f"h_ps{b}{q}", [P, 2, CR]) for q in range(2)] for b in range(2)]
        f_ps = ph.ps("f_ps", [P, H])
        s_w, s_d, s_adiag, s_fold, s_wc, s_gT, s_gTs, s_h, s_ent, s_c, s_arg, s_ex, s_out, s_z, s_zd, s_gend = (
            ph.sem(n) for n in ("w", "d", "adiag", "fold", "wc", "gT", "gTs", "h", "ent", "c", "arg", "ex", "out", "z", "zd", "gend"))
        s_g = ph.sem("g")
        s_in = [ph.sem(f"in{b}") for b in range(2)]
        s_st = [ph.sem(f"st{b}") for b in range(2)]
        block = ph.block()
        srow_ent = lambda b: srow[:, b, 0:C]

        @block.gpsimd
        def _(pool):
            pool.memset(zero[:, :], 0.0).then_inc(s_z, 1)

            def take(t, b):
                if past(t, 2):
                    pool.wait_ge(s_gT, t - 1)
                pool.tensor_copy(g[:, b, :, :], acc_h[:, ds(t * 4, 4), 0:C]).then_inc(s_g, 1)

            pipeline(pool, TILES, 2, [(0, take)])

        @block.sync
        def _(sp):
            sp.dma_start(w_c[:, 0:C], T.W_cross).then_inc(s_w, 16)
            sp.dma_start(w_cT[:, :], T.W_crossT).then_inc(s_w, 16)
            sp.dma_start(att[:, :], T.att).then_inc(s_w, 16)
            sp.dma_start(blang[:, :], T.bias_lang.rearrange("(a c) -> a c", a=1).to_broadcast([P, C])).then_inc(s_w, 16)
            sp.dma_start(valid[:, :, :], T.valid.rearrange("(t p) r -> p t r", p=P)).then_inc(s_w, 16)

            def load(t, b):
                if past(t, 2):
                    sp.wait_ge(s_out, t - 1)
                sp.dma_start(x[:, b, :], T.x[ds(t * P, P), :]).then_inc(s_in[b], 16)
                sp.dma_start(srow[:, b, :], T.srow[ds(t * P, P), :]).then_inc(s_in[b], 16)

            def store(t, b):
                sp.wait_ge(s_out, t + 1)
                sp.dma_start(T.x1[ds(t * P, P), :], out[:, b, :]).then_inc(s_st[b], 16)

            pipeline(sp, TILES, 2, [(1, store), (0, load)])
            sp.wait_ge(s_z, 1)
            for tab in T.sums:
                rows = tab.rearrange("(a p f) c -> a p (f c)", p=P, f=4)
                for a in range(rows.shape[0]):
                    sp.dma_start(rows[a, :, :], zero[:, :]).then_inc(s_zd, 16)
            sp.wait_ge(s_zd, 16 * 2 * rows.shape[0])
            for b in range(2):
                sp.wait_ge(s_st[b], 16 * (TILES // 2))

        @block.vector
        def _(dve):
            dve.wait_ge(s_w, 80)
            dve.tensor_scalar(adiag[:, :], K.headmask[:, :], att[:, 2 * R:2 * R + 1], None, ALU.mult).then_inc(s_adiag, 1)
            dve.tensor_scalar(hide[:, :, :], valid[:, :, :], 1.0, BIG, ALU.subtract, ALU.mult).then_inc(s_adiag, 1)
            dve.wait_ge(s_fold, 1)
            dve.tensor_copy(w_c[:, C:CR], f_ps[:, :]).then_inc(s_wc, 1)
            dve.wait_ge(s_adiag, 2)
            c, e = Chain(dve, s_c, 6), Chain(dve, s_d, 4)

            def logits(t, b):
                dve.wait_ge(s_ent, t + 1)
                dve.wait_ge(s_in[b], filled(t, b, 2, 32))
                c.group(t)
                c.mark(dve.tensor_copy(ls[:, b, 0, :], srow[:, b, C:CR]))
                c.link(dve.tensor_copy(ent[:, b, 0, :], srow_ent(b)))
                c.link(dve.tensor_tensor(t1[:, :, :], ls[:, b, :, :],
                                         srow[:, b, CR:CR + H].unsqueeze(1).to_broadcast([P, M, H]), ALU.add))
                c.link(dve.scalar_tensor_tensor(t1[:, :, :], t1[:, :, :], SLOPE0, t1[:, :, :], ALU.mult, ALU.max))
                c.link(dve.tensor_tensor(t1[:, 1:M, :], t1[:, 1:M, :],
                                         hide[:, ds(t, 1), :].rearrange("p a r -> p (a r)").unsqueeze(2).to_broadcast([P, R, H]), ALU.add))
                c.link(dve.tensor_reduce(top[:, :], t1[:, :, :].rearrange("p m h -> p h m"), AX.X, ALU.max))
                dve.tensor_tensor(al[:, b, :, :], t1[:, :, :], top[:, :].unsqueeze(1).to_broadcast([P, M, H]),
                                  ALU.subtract).then_inc(s_arg, 1)

            def mix(t, b):
                dve.wait_ge(s_ex, t + 1)
                e.group(t)
                e.link(dve.tensor_reduce(den[:, :], ex[:, b, :, :].rearrange("p m h -> p h m"), AX.X, ALU.add))
                e.link(dve.reciprocal(den[:, :], den[:, :]))
                e.link(dve.tensor_tensor(ex[:, b, :, :], ex[:, b, :, :], den[:, :].unsqueeze(1).to_broadcast([P, M, H]), ALU.mult))
                e.link(dve.tensor_tensor(prod[:, :, :].rearrange("p m (h d) -> p (m h) d", h=H),
                                         ent[:, b, :, :].rearrange("p m (h d) -> p (m h) d", h=H),
                                         flat(ex[:, b, :, :]).unsqueeze(2).to_broadcast([P, M * H, D]), ALU.mult))
                if past(t, 2):
                    dve.wait_ge(s_st[b], (t - b) * 8)
                dve.tensor_reduce(out[:, b, :], prod[:, :, :].rearrange("p m c -> p c m"), AX.X, ALU.add).then_inc(s_gend, 1)
                dve.wait_ge(s_gend, 2 * t + 1)
                dve.tensor_tensor(out[:, b, :], out[:, b, :], x[:, b, :], ALU.add).then_inc(s_gend, 1)
                dve.wait_ge(s_gend, 2 * t + 2)
                dve.tensor_tensor(out[:, b, :], out[:, b, :], blang[:, :], ALU.add).then_inc(s_out, 1)

            pipeline(dve, TILES, 2, [(1, mix), (0, logits)])

        @block.scalar
        def _(act):
            def move(t, b):
                act.wait_ge(s_gT, t + 1)
                if past(t, 2):
                    act.wait_ge(s_h, t - 1)
                act.activation(gT[:, b, :], gT_ps[b][:, :], ACT.Copy).then_inc(s_gTs, 1)

            def entries(t, b):
                act.wait_ge(s_h, t + 1)
                if past(t, 2):
                    act.wait_ge(s_out, t - 1)
                for q in range(2):
                    act.activation(ent[:, b, 1 + 2 * q:3 + 2 * q, :], h_ps[b][q][:, :, 0:C], ACT.Copy)
                    last = act.activation(ls[:, b, 1 + 2 * q:3 + 2 * q, :], h_ps[b][q][:, :, C:CR], ACT.Copy)
                last.then_inc(s_ent, 1)

            def exponentials(t, b):
                act.wait_ge(s_arg, t + 1)
                if past(t, 2):
                    act.wait_ge(s_out, t - 1)
                act.activation(ex[:, b, :, :], al[:, b, :, :], ACT.Exp).then_inc(s_ex, 1)

            pipeline(act, TILES, 2, [(1, exponentials), (0, move), (0, entries)])

        @block.tensor
        def _(pe):
            pe.wait_ge(s_w, 80)
            pe.wait_ge(s_adiag, 1)
            pe.matmul(f_ps[:, :], w_cT[:, :], adiag[:, :], start=True, stop=True).then_inc(s_fold, 1)
            pe.wait_ge(s_wc, 1)

            def transpose(t, b):
                if past(t, 2):
                    pe.wait_ge(s_gTs, t - 1)
                pe.wait_ge(s_g, t + 1)
                for u in range(4):
                    last = pe.transpose(gT_ps[b][:, u * P:(u + 1) * P], g[:, b, u, :], K.ident[:, :])
                last.then_inc(s_gT, 1)

            def project(t, b):
                pe.wait_ge(s_gTs, t + 1)
                if past(t, 2):
                    pe.wait_ge(s_ent, t - 1)
                g4 = gT[:, b, :].rearrange("f (n r) -> f r n", r=R)
                for r in range(R):
                    last = pe.matmul(h_ps[b][r // 2][:, r % 2, :], g4[:, r, :], w_c[:, :], start=True, stop=True)
                last.then_inc(s_h, 1)

            pipeline(pe, TILES, 2, [(1, project), (0, transpose)])


def edge_inputs(nc, K, T, h1T):
    with Phase(nc, "edgein") as ph:
        x = ph.sb("x", [P, TILES, C])
        stats = ph.sb("stats", [P, 2, 6])
        mv = ph.sb("mv", [P, 2, 2])
        mean = ph.sb("mean", [P, TILES])
        rstd = ph.sb("rstd", [P, TILES])
        nmr = ph.sb("nmr", [P, TILES])
        w = ph.sb("w", [P, 2, HID])
        h = ph.sb("h", [P, 2, C])
        hT = ph.sb("hT", [P, 2, P])
        ab = ph.sb("ab", [P, 2, 2 * HID])
        hT_ps = [ph.ps(f"hT_ps{b}", [P, P]) for b in range(2)]
        ab_ps = [ph.ps(f"ab_ps{b}", [P, 2 * HID]) for b in range(2)]
        s_w, s_x, s_v, s_stat, s_var, s_sd, s_norm, s_h, s_hT, s_hTs, s_ab, s_abs, s_prep = (
            ph.sem(n) for n in ("w", "x", "v", "stat", "var", "sd", "norm", "h", "hT", "hTs", "ab", "abs", "prep"))
        s_st = [ph.sem(f"st{b}") for b in range(2)]
        valid = ph.sb("valid", [P, STEPS])
        inside = ph.sb("inside", [P, STEPS])
        srci = ph.sb("srci", [P, STEPS], I32)
        part = ph.sb("part", [P, STEPS], I32)
        block = ph.block()

        @block.sync
        def _(sp):
            sp.dma_start(x[:, :, :], T.x1.rearrange("(t p) c -> p t c", p=P)).then_inc(s_x, 16)
            sp.dma_start(w[:, :, :], T.We1[0:2 * C, :].rearrange("(s i) o -> i s o", s=2)).then_inc(s_w, 16)

            def store(t, b):
                sp.wait_ge(s_abs, t + 1)
                sp.dma_start(T.ab[ds(t * P, P), :], ab[:, b, :]).then_inc(s_st[b], 16)

            pipeline(sp, TILES, 2, [(0, store)])
            for b in range(2):
                sp.wait_ge(s_st[b], 16 * (TILES // 2))

        @block.vector
        def _(dve):
            L = Links(dve, s_v)
            dve.wait_ge(s_x, 16)
            chain = Chain(dve, s_stat, 4)

            def statistics(t, b):
                chain.group(t)
                chain.link(dve.bn_stats(stats[:, b, :], x[:, ds(t, 1), :].rearrange("p a c -> p (a c)")))
                settle(dve, K)
                chain.link(dve.bn_aggr(mv[:, b, :], stats[:, b, :]))
                chain.mark(dve.tensor_copy(mean[:, ds(t, 1)], mv[:, b, 0:1]))
                chain.mark(dve.tensor_scalar(rstd[:, ds(t, 1)], mv[:, b, 1:2], EPS, None, ALU.add))

            pipeline(dve, TILES, 2, [(0, statistics)])
            dve.wait_ge(s_stat, 4 * TILES)
            dve.sem_inc(s_var, 1)
            dve.wait_ge(s_sd, 1)
            L.link(dve.reciprocal(rstd[:, :], rstd[:, :]))
            dve.scalar_tensor_tensor(nmr[:, :], mean[:, :], -1.0, rstd[:, :], ALU.mult, ALU.mult).then_inc(s_norm, 1)

            def evacuate(t, b):
                dve.wait_ge(s_hT, t + 1)
                if past(t, 2):
                    dve.wait_ge(s_ab, t - 1)
                dve.tensor_copy(h1T[:, ds(t * P, P)], hT_ps[b][:, :])
                dve.tensor_copy(hT[:, b, :], hT_ps[b][:, :]).then_inc(s_hTs, 1)

            pipeline(dve, TILES, 2, [(0, evacuate)])
            L.mark(dve.tensor_scalar(valid[:, :], K.loc[:, :], 0.0, None, ALU.is_ge))
            L.link(dve.tensor_scalar(inside[:, :], K.loc[:, :], float(WIN), None, ALU.is_lt))
            L.link(dve.tensor_tensor(valid[:, :], valid[:, :], inside[:, :], ALU.mult))
            L.link(dve.scalar_tensor_tensor(K.srcv[:, :], K.src[:, :], 1.0, valid[:, :], ALU.add, ALU.mult))
            L.mark(dve.scalar_tensor_tensor(K.rowd[:, :], K.src[:, :], K.trash[:, 0:1], valid[:, :], ALU.subtract, ALU.mult))
            L.link(dve.tensor_copy(srci[:, :], K.srcv[:, :]))
            L.link(dve.tensor_scalar(part[:, :], srci[:, :], 7, None, ALU.arith_shift_right))
            L.link(dve.tensor_copy(K.src_hi[:, :], part[:, :]))
            L.link(dve.tensor_scalar(part[:, :], srci[:, :], P - 1, None, ALU.bitwise_and))
            L.link(dve.tensor_copy(K.src_lo[:, :], part[:, :]))

        @block.scalar
        def _(act):
            act.wait_ge(s_var, 1)
            act.activation(rstd[:, :], rstd[:, :], ACT.Sqrt).then_inc(s_sd, 1)
            act.wait_ge(s_norm, 1)

            def normalize(t, b):
                if past(t, 2):
                    act.wait_ge(s_hT, t - 1)
                act.activation(h[:, b, :], x[:, ds(t, 1), :].rearrange("p a c -> p (a c)"), ACT.Relu,
                               bias=nmr[:, ds(t, 1)], scale=rstd[:, ds(t, 1)]).then_inc(s_h, 1)

            def evacuate(t, b):
                act.wait_ge(s_ab, t + 1)
                if past(t, 2):
                    act.wait_ge(s_st[b], (t - b) * 8)
                act.activation(ab[:, b, :], ab_ps[b][:, :], ACT.Copy).then_inc(s_abs, 1)

            pipeline(act, TILES, 2, [(0, normalize), (1, evacuate)])

        @block.tensor
        def _(pe):
            pe.wait_ge(s_w, 16)

            def transpose(t, b):
                pe.wait_ge(s_h, t + 1)
                if past(t, 2):
                    pe.wait_ge(s_hTs, t - 1)
                pe.transpose(hT_ps[b][:, :], h[:, b, :], K.ident[:, :]).then_inc(s_hT, 1)

            def products(t, b):
                pe.wait_ge(s_hTs, t + 1)
                if past(t, 2):
                    pe.wait_ge(s_abs, t - 1)
                pe.matmul(ab_ps[b][:, :], hT[:, b, :], flat(w[:, :, :]), start=True, stop=True).then_inc(s_ab, 1)

            pipeline(pe, TILES, 2, [(0, transpose), (0, products)])


def edge_messages(nc, K, T, fwd):
    with Phase(nc, "msg") as ph:
        U, RG = 4, 4
        GROUPS = STEPS // U
        SUM_LAG, ADD_LAG = 2, 3
        idx = ph.sb("idx", [P, RG, U], I32)
        sidx = ph.sb("sidx", [P, RG, U], I32)
        srcv = ph.sb("srcv", [P, RG, U])
        shi = ph.sb("shi", [P, RG, U], BF16)
        slo = ph.sb("slo", [P, RG, U], BF16)
        dup = ph.sb("dup", [P, RG, U])
        rowf = ph.sb("rowf", [P, U])
        onehot = ph.sb("onehot", [P, RG, U, WIN])
        same = ph.sb("same", [P, 2, U, P])
        junk = ph.sb("junk", [P, U, P])
        ga = ph.sb("ga", [P, RG, U, 2 * HID])
        lt = ph.sb("lt", [P, RG, U, P])
        rw = ph.sb("rw", [P, 2, U, 2 * HID])
        xs = ph.sb("xs", [P, 2, 2 * HID])
        hid = ph.sb("hid", [P, 2, U, 2 * HID])
        bsum = ph.sb("bsum", [P, 2, U, HID])
        oT_ps = ph.ps("oT_ps", [WIN, U * P])
        src_ps = ph.ps("src_ps", [P, U, P])
        pre_ps = [ph.ps(f"pre_ps{b}", [P, 2 * HID]) for b in range(2)]
        fwd_ps = [ph.ps(f"fwd_ps{b}", [P, 2 * WIN]) for b in range(2)]
        bwd_ps = [ph.ps(f"bwd_ps{b}", [P, HID]) for b in range(2)]
        s_ga = [ph.sem(f"ga{b}") for b in range(RG)]
        s_ef = [ph.sem(f"ef{b}") for b in range(RG)]
        s_rw = [ph.sem(f"rw{b}") for b in range(2)]
        s_sum = [ph.sem(f"sum{u}") for u in range(U)]
        (s_w, s_idx, s_oh, s_tr, s_oT, s_same, s_row, s_pre, s_x, s_hid, s_edge, s_acc, s_bs, s_rc) = (
            ph.sem(n) for n in ("w", "idx", "oh", "tr", "oT", "same", "row", "pre", "x", "hid", "edge", "acc", "bs", "rc"))
        block = ph.block()

        @block.sync
        def _(sp):
            for b in range(2):
                for u in range(U):
                    for q in range(2):
                        sp.dma_start(rw[WIN:P, b, u, q * HID:(q + 1) * HID], T.We1[2 * C:2 * C + EF, :]).then_inc(s_w, 16)
            sp.wait_ge(s_w, 16 * 4 * U)

            def features(j, b):
                e = registers(nc, sp, mybir.EngineType.SP, K.reg_e, j * U, U, N_EDGES)
                if past(j, RG):
                    sp.wait_ge(s_pre, (j - RG + 1) * U)
                    settle(sp, K)
                for u in range(U):
                    sp.dma_start(lt[WIN:P, b, u, :], T.efT[:, ds(e[u], P)]).then_inc(s_ef[b], 16)

            def windows(j, b):
                w = registers(nc, sp, mybir.EngineType.SP, K.reg_w, j * U, U, WINDOWS - 1)
                if past(j, 2):
                    sp.wait_ge(s_pre, (j - 1) * U)
                    settle(sp, K)
                for u in range(U):
                    sp.dma_start(rw[0:WIN, b % 2, u, :], T.ab[ds(w[u] * WIN, WIN), :]).then_inc(s_rw[b % 2], 16)

            pipeline(sp, GROUPS, RG, [(0, features), (0, windows)])

        @block.gpsimd
        def _(pool):
            def scatter(j, b, u):
                if u == 0:
                    pool.wait_ge(s_row, j + 1)
                pool.wait_ge(s_bs, j * U + u + 1)
                if u >= 2:
                    pool.wait_ge(s_sum[u - 2], (j + 1) * 16)
                elif past(j, 1):
                    pool.wait_ge(s_sum[u + 2], j * 16)
                settle(pool, K)
                pool.indirect_dma_start(T.sums[u % 2], bass.IndirectOffsetOnAxis(ap=sidx[:, b, u:u + 1], axis=0),
                                        bsum[:, b % 2, u, :], None, compute_op=ALU.add).then_inc(s_sum[u], 16)

            def gather(j, b, u):
                if u == 0:
                    pool.wait_ge(s_idx, j + 1)
                if past(j, RG):
                    pool.wait_ge(s_x, (j - RG) * U + u + 1)
                settle(pool, K)
                pool.indirect_dma_start(ga[:, b, u, :], None, T.ab,
                                        bass.IndirectOffsetOnAxis(ap=idx[:, b, u:u + 1], axis=0)).then_inc(s_ga[b], 16)

            stages = []
            for u in range(U):
                stages += [(5, lambda j, b, u=u: scatter(j, b, u)), (0, lambda j, b, u=u: gather(j, b, u))]
            pipeline(pool, GROUPS, RG, stages)
            for u in range(U):
                pool.wait_ge(s_sum[u], 16 * GROUPS)

        @block.vector
        def _(dve):
            dve.memset(fwd[:, :, :, :], 0.0).then_inc(s_acc, 1)
            dve.wait_ge(s_acc, 1)
            rc = Chain(dve, s_rc, 1)

            def indices(j, b):
                dve.tensor_copy(idx[:, b, :], K.src[:, ds(j * U, U)]).then_inc(s_idx, 1)

            def hots(j, b):
                if past(j, RG):
                    dve.wait_ge(s_edge, (j - RG + 1) * U)
                k = ds(j * U, U)
                dve.tensor_copy(shi[:, b, :], K.src_hi[:, k])
                dve.tensor_copy(slo[:, b, :], K.src_lo[:, k])
                dve.tensor_copy(srcv[:, b, :], K.srcv[:, k])
                dve.tensor_tensor(onehot[:, b, :, :], K.ramp[:, 0:WIN].unsqueeze(1).to_broadcast([P, U, WIN]),
                                  K.loc[:, k].unsqueeze(2).to_broadcast([P, U, WIN]), ALU.is_equal).then_inc(s_oh, 1)

            def compare(j, b, u):
                if u == 0:
                    dve.wait_ge(s_tr, j + 1)
                    dve.wait_ge(s_oh, j + 1)
                if past(j, 2):
                    dve.wait_ge(s_edge, (j - 2) * U + u + 1)
                dve.tensor_scalar(same[:, b % 2, u, :], src_ps[:, u, :], srcv[:, b, u:u + 1], None, ALU.is_equal)

            def count(j, b, u):
                dve.scalar_tensor_tensor(junk[:, u, :], src_ps[:, u, :], srcv[:, b, u:u + 1], K.below[:, :],
                                         ALU.is_equal, ALU.mult, accum_out=dup[:, b, u:u + 1]).then_inc(s_same, 1)

            def rows(j, b):
                if isinstance(j, int) and j == 0:
                    for u in range(U):
                        compare(j, b, u)
                        count(j, b, u)
                dve.wait_ge(s_same, (j + 1) * U)
                rc.group(j)
                rc.link(dve.scalar_tensor_tensor(rowf[:, :], dup[:, b, :], 0.0, K.rowd[:, ds(j * U, U)], ALU.is_equal, ALU.mult))
                if past(j, RG):
                    for u in range(U):
                        dve.wait_ge(s_sum[u], (j - RG + 1) * 16)
                dve.tensor_scalar(sidx[:, b, :], rowf[:, :], K.trash[:, 0:1], None, ALU.add).then_inc(s_row, 1)

            def add(n, u, w):
                dve.wait_ge(s_edge, n + 1)
                dve.wait_ge(s_acc, n + 1)
                dst = fwd[:, ds(w, 1), :, :].rearrange("f a c n -> f (a c n)")
                dve.tensor_tensor(dst, dst, fwd_ps[u % 2][:, :], ALU.add).then_inc(s_acc, 1)

            def steps(j, b):
                first, final = isinstance(j, int) and j == 0, isinstance(j, int) and j == GROUPS - 1
                skip = ADD_LAG if first else 0
                w = registers(nc, dve, mybir.EngineType.DVE, K.reg_w, j * U - ADD_LAG + skip, U - skip, WINDOWS - 1)
                for u in range(U):
                    n = j * U + u
                    if u >= skip:
                        add(n - ADD_LAG, (u - ADD_LAG) % U, w[u - skip])
                    if u == 0:
                        dve.wait_ge(s_ga[b], filled(j, b, RG, 16 * U))
                    dve.wait_ge(s_pre, n + 1)
                    if past(j, 1) or u >= 2:
                        dve.wait_ge(s_hid, n - 1)
                    dve.tensor_tensor(xs[:, u % 2, 0:HID], pre_ps[u % 2][:, 0:HID], ga[:, b, u, HID:2 * HID], ALU.add)
                    dve.tensor_tensor(xs[:, u % 2, HID:2 * HID], pre_ps[u % 2][:, HID:2 * HID], ga[:, b, u, 0:HID],
                                      ALU.add).then_inc(s_x, 1)
                    if not final:
                        compare(j + 1, (b + 1) % RG, u)
                        count(j + 1, (b + 1) % RG, u)
                    dve.wait_ge(s_x, n + 1)
                    if past(j, 2):
                        dve.wait_ge(s_edge, (j - 2) * U + u + 1)
                    dve.scalar_tensor_tensor(hid[:, b % 2, u, :], xs[:, u % 2, :], SLOPE1, xs[:, u % 2, :],
                                             ALU.mult, ALU.max).then_inc(s_hid, 1)

            pipeline(dve, GROUPS, RG, [(0, indices), (2, steps), (1, rows), (0, hots)])
            w = registers(nc, dve, mybir.EngineType.DVE, K.reg_w, STEPS - ADD_LAG, ADD_LAG, WINDOWS - 1)
            for n in range(STEPS - ADD_LAG, STEPS):
                add(n, n % U, w[n - STEPS + ADD_LAG])
            dve.wait_ge(s_acc, STEPS + 1)

        @block.scalar
        def _(act):
            def move(j, b):
                act.wait_ge(s_tr, j + 1)
                if past(j, RG):
                    act.wait_ge(s_pre, (j - RG + 1) * U)
                act.activation(lt[0:WIN, b, :, :], oT_ps[:, :].rearrange("n (u p) -> n u p", u=U), ACT.Copy).then_inc(s_oT, 1)

            def sums(j, b):
                for u in range(U):
                    act.wait_ge(s_edge, j * U + u + 1)
                    if past(j, 2):
                        act.wait_ge(s_sum[u], (j - 1) * 16)
                    act.activation(bsum[:, b % 2, u, :], bwd_ps[u % 2][:, :], ACT.Copy).then_inc(s_bs, 1)

            pipeline(act, GROUPS, RG, [(2, sums), (0, move)])

        @block.tensor
        def _(pe):
            pe.wait_ge(s_w, 16 * 4 * U)

            def transpose(j, b):
                pe.wait_ge(s_oh, j + 1)
                if past(j, 1):
                    pe.wait_ge(s_oT, j)
                    pe.wait_ge(s_same, j * U)
                settle(pe, K)
                for u in range(U):
                    pe.transpose(oT_ps[:, u * P:(u + 1) * P], onehot[:, b, u, :], K.ident[:, :])
                for u in range(U):
                    pe.matmul(src_ps[:, u, :], shi[:, b, u:u + 1].to_broadcast([P, P]), K.identb128[:, :], start=True, stop=False)
                    last = pe.matmul(src_ps[:, u, :], slo[:, b, u:u + 1].to_broadcast([P, P]), K.identb[:, :], start=False, stop=True)
                last.then_inc(s_tr, 1)

            def after(n, j, b, u):
                pe.wait_ge(s_hid, n + 1)
                pe.wait_ge(s_same, n + 1)
                if past(j, 1) or u >= 2:
                    pe.wait_ge(s_acc, n)
                    pe.wait_ge(s_bs, n - 1)
                for q in range(2):
                    pe.matmul(fwd_ps[u % 2][:, q * WIN:(q + 1) * WIN], hid[:, b % 2, u, HID + q * P:HID + (q + 1) * P],
                              onehot[:, b, u, :], start=True, stop=True)
                pe.matmul(bwd_ps[u % 2][:, :], same[:, b % 2, u, :], hid[:, b % 2, u, 0:HID],
                          start=True, stop=True).then_inc(s_edge, 1)

            def steps(j, b):
                pe.wait_ge(s_oT, j + 1)
                pe.wait_ge(s_ef[b], filled(j, b, RG, 16 * U))
                pe.wait_ge(s_rw[b % 2], (j // 2 + 1) * 16 * U if isinstance(j, int) else (j - b % 2) * 8 * U + 16 * U)
                for u in range(U):
                    n = j * U + u
                    if past(j, 1) or u >= 2:
                        pe.wait_ge(s_x, n - 1)
                    pe.matmul(pre_ps[u % 2][:, :], lt[:, b, u, :], rw[:, b % 2, u, :], start=True, stop=True).then_inc(s_pre, 1)
                    if u >= SUM_LAG:
                        after(n - SUM_LAG, j, b, u - SUM_LAG)
                    elif past(j, 1):
                        after(n - SUM_LAG, j - 1, (b - 1) % RG, u - SUM_LAG + U)
                    if u == 0 and not (isinstance(j, int) and j == GROUPS - 1):
                        transpose(j + 1, (b + 1) % RG)

            transpose(0, 0)
            pipeline(pe, GROUPS, RG, [(1, steps)])
            for n in range(STEPS - SUM_LAG, STEPS):
                after(n, GROUPS - 1, (GROUPS - 1) % RG, n % U)


def outputs(nc, K, T, fwd, h1T):
    with Phase(nc, "out") as ph:
        tab = ph.sb("tab", [P, 2, 2, HID])
        bsum = ph.sb("bsum", [P, 2, HID])
        x = ph.sb("x", [P, 2, C])
        hsum = ph.sb("hsum", [P, 2, 2, P])
        red = ph.sb("red", [P, 2, P])
        z = ph.sb("z", [P, 2, 2, P])
        zl = ph.sb("zl", [P, 2, 2, P])
        y = ph.sb("y", [P, 2, C])
        we2 = ph.sb("we2", [P, 2, C])
        wn1 = ph.sb("wn1", [P, 2, HID])
        wn2 = ph.sb("wn2", [P, 2, C])
        bT_ps = [ph.ps(f"bT_ps{b}", [P, 2, P]) for b in range(2)]
        red_ps = [ph.ps(f"red_ps{b}", [P, P]) for b in range(2)]
        z_ps = [ph.ps(f"z_ps{b}", [P, 2, P]) for b in range(2)]
        y_ps = [ph.ps(f"y_ps{b}", [P, C]) for b in range(2)]
        s_in = [ph.sem(f"in{b}") for b in range(2)]
        s_xin = [ph.sem(f"xin{b}") for b in range(2)]
        s_st = [ph.sem(f"st{b}") for b in range(2)]
        s_w, s_b, s_bT, s_hs, s_red, s_reds, s_z, s_zs, s_zl, s_y, s_out = (
            ph.sem(n) for n in ("w", "b", "bT", "hs", "red", "reds", "z", "zs", "zl", "y", "o"))
        block = ph.block()

        @block.sync
        def _(sp):
            sp.dma_start(we2[:, :, :], T.We2.rearrange("(q i) o -> i q o", q=2)).then_inc(s_w, 16)
            sp.dma_start(wn1[:, :, :], T.Wn1.rearrange("(q i) o -> i q o", q=2)).then_inc(s_w, 16)
            sp.dma_start(wn2[:, :, :], T.Wn2.rearrange("(q i) o -> i q o", q=2)).then_inc(s_w, 16)

            def load(t, b):
                if past(t, 2):
                    sp.wait_ge(s_b, t - 1)
                for q in range(2):
                    sp.dma_start(tab[:, b, q, :], T.sums[q][ds(t * P, P), :]).then_inc(s_in[b], 16)

            def load_x(t, b):
                if past(t, 2):
                    sp.wait_ge(s_out, t - 1)
                sp.dma_start(x[:, b, :], T.x1[ds(t * P, P), :]).then_inc(s_xin[b], 16)

            def store(t, b):
                sp.wait_ge(s_out, t + 1)
                sp.dma_start(T.out[ds(t * P, P), :], y[:, b, :]).then_inc(s_st[b], 16)

            pipeline(sp, TILES, 2, [(0, load), (3, load_x), (5, store)])
            for b in range(2):
                sp.wait_ge(s_st[b], 16 * (TILES // 2))

        @block.vector
        def _(dve):
            def gather(t, b):
                dve.wait_ge(s_in[b], filled(t, b, 2, 32))
                if past(t, 2):
                    dve.wait_ge(s_bT, t - 1)
                dve.tensor_tensor(bsum[:, b, :], tab[:, b, 0, :], tab[:, b, 1, :], ALU.add).then_inc(s_b, 1)

            def both(t, b):
                dve.wait_ge(s_bT, t + 1)
                if past(t, 2):
                    dve.wait_ge(s_red, t - 1)
                for q in range(2):
                    last = dve.tensor_tensor(hsum[:, b, q, :].rearrange("f (w n) -> f w n", n=WIN),
                                             bT_ps[b][:, q, :].rearrange("f (w n) -> f w n", n=WIN),
                                             fwd[:, ds(t * 2, 2), q, :], ALU.add)
                last.then_inc(s_hs, 1)

            def activate(t, b):
                dve.wait_ge(s_zs, t + 1)
                if past(t, 2):
                    dve.wait_ge(s_y, t - 1)
                dve.scalar_tensor_tensor(zl[:, b, :, :], z[:, b, :, :], SLOPE1, z[:, b, :, :], ALU.mult, ALU.max).then_inc(s_zl, 1)

            def residual(t, b):
                dve.wait_ge(s_y, t + 1)
                dve.wait_ge(s_xin[b], filled(t, b, 2, 16))
                if past(t, 2):
                    dve.wait_ge(s_st[b], (t - b) * 8)
                dve.tensor_tensor(y[:, b, :], y_ps[b][:, :], x[:, b, :], ALU.add).then_inc(s_out, 1)

            dve.wait_ge(s_w, 48)
            pipeline(dve, TILES, 2, [(4, residual), (3, activate), (1, both), (0, gather)])

        @block.scalar
        def _(act):
            def reduced(t, b):
                act.wait_ge(s_red, t + 1)
                if past(t, 2):
                    act.wait_ge(s_z, t - 1)
                act.activation(red[:, b, :], red_ps[b][:, :], ACT.Copy).then_inc(s_reds, 1)

            def hidden(t, b):
                act.wait_ge(s_z, t + 1)
                if past(t, 2):
                    act.wait_ge(s_zl, t - 1)
                act.activation(z[:, b, :, :], z_ps[b][:, :, :], ACT.Copy).then_inc(s_zs, 1)

            pipeline(act, TILES, 2, [(1, hidden), (0, reduced)])

        @block.tensor
        def _(pe):
            pe.wait_ge(s_w, 48)

            def transpose(t, b):
                pe.wait_ge(s_b, t + 1)
                if past(t, 2):
                    pe.wait_ge(s_hs, t - 1)
                for q in range(2):
                    last = pe.transpose(bT_ps[b][:, q, :], bsum[:, b, q * P:(q + 1) * P], K.ident[:, :])
                last.then_inc(s_bT, 1)

            def reduce(t, b):
                pe.wait_ge(s_hs, t + 1)
                if past(t, 2):
                    pe.wait_ge(s_reds, t - 1)
                for q in range(2):
                    last = pe.matmul(red_ps[b][:, :], we2[:, q, :], hsum[:, b, q, :], start=(q == 0), stop=(q == 1))
                last.then_inc(s_red, 1)

            def hidden(t, b):
                pe.wait_ge(s_reds, t + 1)
                if past(t, 2):
                    pe.wait_ge(s_zs, t - 1)
                for q in range(2):
                    pe.matmul(z_ps[b][:, q, :], wn1[:, 0, q * P:(q + 1) * P], h1T[:, ds(t * P, P)], start=True, stop=False)
                    last = pe.matmul(z_ps[b][:, q, :], wn1[:, 1, q * P:(q + 1) * P], red[:, b, :], start=False, stop=True)
                last.then_inc(s_z, 1)

            def output(t, b):
                pe.wait_ge(s_zl, t + 1)
                if past(t, 2):
                    pe.wait_ge(s_out, t - 1)
                for q in range(2):
                    last = pe.matmul(y_ps[b][:, :], zl[:, b, q, :], wn2[:, q, :], start=(q == 0), stop=(q == 1))
                last.then_inc(s_y, 1)

            pipeline(pe, TILES, 2, [(3, output), (2, hidden), (1, reduce), (0, transpose)])


class Namespace:
    pass


def build(nc, T):
    with Phase(nc, "k") as ph:
        K = Namespace()
        K.ramp, K.part, K.grid = ph.sb("ramp", [P, 256]), ph.sb("part", [P, 1]), ph.sb("grid", [P, KC])
        K.ident, K.below, K.ones = ph.sb("ident", [P, P]), ph.sb("below", [P, P]), ph.sb("ones", [P, P])
        K.identb, K.identb128 = ph.sb("identb", [P, P], BF16), ph.sb("identb128", [P, P], BF16)
        K.headmask, K.trash = ph.sb("headmask", [P, H]), ph.sb("trash", [P, 1])
        K.reg_w, K.reg_e = ph.sb("reg_w", [1, P * KC], I32), ph.sb("reg_e", [1, P * KC], I32)
        K.loc, K.src = ph.sb("loc", [P, STEPS]), ph.sb("src", [P, STEPS], I32)
        K.passed = ph.sem("passed")
        constants(nc, K)
        with Phase(nc, "l0") as l0:
            K.key, K.typ, K.idx = l0.sb("key", [P, STEPS]), l0.sb("typ", [P, STEPS]), l0.sb("idx", [P, STEPS], I32)
            with Phase(nc, "ed") as e:
                K.wbase, K.wstep_i = e.sb("wbase", [P, STEPS]), e.sb("wstep_i", [P, STEPS], I32)
                K.ed = e.sb("ed", [WIN, WSLOTS, R * H])
                schedule(nc, K, T)
                node_inputs(nc, K, T)
                relation_maxima(nc, K, T)
            acc = l0.sb("acc", [P, WSLOTS, 2, XR])
            relation_attention(nc, K, T, acc)
            node_update(nc, K, T, acc)
        with Phase(nc, "l1") as l1:
            K.srcv, K.rowd = l1.sb("srcv", [P, STEPS]), l1.sb("rowd", [P, STEPS])
            K.src_hi, K.src_lo = l1.sb("src_hi", [P, STEPS], BF16), l1.sb("src_lo", [P, STEPS], BF16)
            h1T = l1.sb("h1T", [P, NP])
            edge_inputs(nc, K, T, h1T)
            fwd = l1.sb("fwd", [P, WSLOTS, 2, WIN])
            edge_messages(nc, K, T, fwd)
            outputs(nc, K, T, fwd, h1T)


def kernel(x, src, dst, edge_attr_64, edge_type_4, L0_gnn_W_rel, L0_gnn_att_src_rel, L0_gnn_att_dst_rel, L0_gnn_bias_rel,
           L0_gnn_W_self, L0_gnn_W_cross, L0_gnn_att_src_lang, L0_gnn_att_dst_lang, L0_gnn_bias_lang,
           L1_gnn_We1, L1_gnn_We2, L1_gnn_Wn1, L1_gnn_Wn2):
    import numpy as np
    import concourse.bacc as bacc
    from concourse.bass_utils import run_bass_kernel_spmd as run

    nc = bacc.Bacc("TRN2", target_bir_lowering=False, num_devices=1)
    asn = np.ascontiguousarray
    src, dst, typ = (np.asarray(a).astype(np.int32) for a in (src, dst, edge_type_4))

    rec = np.zeros((EPAD, REC), np.int32)
    rec[:, 1] = rec[:, 3] = rec[:, 4] = PAD_DST
    rec[:N_EDGES, 0], rec[:N_EDGES, 1], rec[:N_EDGES, 2] = src, dst, typ
    rec[1:, 3], rec[:-1, 4] = rec[:-1, 1], rec[1:, 1]
    all_dst = np.full((P * DCOLS,), PAD_DST, np.int32)
    all_dst[:N_EDGES] = dst
    xp = np.zeros((NP, C), np.float32)
    xp[:N_NODES] = x
    efT = np.zeros((EF, EPAD), np.float32)
    efT[:, :N_EDGES] = np.asarray(edge_attr_64).T
    a_s, a_d = (np.asarray(a).reshape(R, C) for a in (L0_gnn_att_src_rel, L0_gnn_att_dst_rel))
    l_s, l_d = (np.asarray(a).reshape(1, C) for a in (L0_gnn_att_src_lang, L0_gnn_att_dst_lang))
    att = asn(np.concatenate([np.stack([a_s, a_d], axis=1).reshape(2 * R, C), l_s, l_d]).T)

    given = {
        "x": xp, "rec": rec, "dst": all_dst.reshape(P, DCOLS), "efT": efT, "att": att,
        "W_rel": asn(L0_gnn_W_rel), "W_relT": asn(np.asarray(L0_gnn_W_rel).transpose(0, 2, 1)),
        "W_self": asn(L0_gnn_W_self), "W_selfT": asn(np.asarray(L0_gnn_W_self).T),
        "W_cross": asn(L0_gnn_W_cross), "W_crossT": asn(np.asarray(L0_gnn_W_cross).T),
        "bias_rel": asn(L0_gnn_bias_rel), "bias_lang": asn(L0_gnn_bias_lang),
        "We1": asn(L1_gnn_We1), "We2": asn(L1_gnn_We2), "Wn1": asn(L1_gnn_Wn1), "Wn2": asn(L1_gnn_Wn2),
    }
    T = Namespace()
    for name, a in given.items():
        T.__dict__[name] = nc.dram_tensor(f"in_{name}", a.shape, mybir.dt.from_np(a.dtype), kind="ExternalInput").ap()
    inner = lambda name, shape, dt=F32: nc.dram_tensor(name, shape, dt, kind="Internal").ap()
    T.sched_w, T.sched_e = inner("sched_w", (P * KC,), I32), inner("sched_e", (P * KC,), I32)
    T.xrel, T.esrc, T.srow = inner("xrel", (R * NP, XR)), inner("esrc", (R * NP, H)), inner("srow", (NP, C + 2 * H))
    T.edm, T.valid = inner("edm", (NP, R * 2 * H)), inner("valid", (NP, R))
    T.x1, T.ab = inner("x1", (NP, C)), inner("ab", (NP, 2 * HID))
    T.sums = [inner(f"sums{q}", (SUM_ROWS, HID)) for q in range(2)]
    T.out = nc.dram_tensor("out", (NP, C), F32, kind="ExternalOutput").ap()
    build(nc, T)
    r = run(nc, [{f"in_{k}": a for k, a in given.items()}], core_ids=[0])
    return r.results[0]["out"][:N_NODES]
```

```python
import concourse.bass as bass
from concourse import mybir
from contextlib import ExitStack

F32, I32, BF16 = mybir.dt.float32, mybir.dt.int32, mybir.dt.bfloat16
ALU = mybir.AluOpType
ACT = mybir.ActivationFunctionType
AX = mybir.AxisListType
ds = bass.ds

P = 128
N_NODES, N_EDGES = 6250, 106250
C = 128
R, H, D = 4, 8, 16
EF = 64
HID = 256
XR = C + H
TILES = 50
NP = TILES * P
WIN = 64
WINDOWS = -(-N_NODES // WIN)
WSLOTS = NP // WIN
G = 8
STEPS = -(-((N_EDGES + (P - 1) * WINDOWS) // P) // (2 * G)) * (2 * G)
BLOCKS = -(-N_EDGES // P)
EPAD = BLOCKS * P + 2 * P
SUM_ROWS = -(-(NP + P) // (4 * P)) * (4 * P)
KC = 8
PAD_DST = 1 << 20
BIG = 1e30
SLOPE0, SLOPE1 = 0.2, 0.01
EPS = 1e-5
REC = 6


def flat(ap):
    return ap.rearrange("p a b -> p (a b)")


class Links:

    def __init__(self, eng, sem):
        self.eng, self.sem, self.n = eng, sem, 0

    def on(self, eng):
        self.eng = eng
        return self

    def mark(self, ins):
        ins.then_inc(self.sem, 1)
        self.n += 1

    def wait(self):
        self.eng.wait_ge(self.sem, self.n)

    def link(self, ins):
        self.mark(ins)
        self.wait()


def ticks(eng, groups, ring, depth, f):
    head = -(-(depth + ring) // ring) * ring
    full = groups - groups % ring
    assert full > head
    for t in range(head):
        f(t, t % ring, lambda skew: t >= skew)
    with eng.Fori(head // ring, full // ring) as i:
        for h in range(ring):
            f(i * ring + h, h, lambda skew: True)
    for t in range(full, groups + depth):
        f(t, t % ring, lambda skew: t - skew < groups)


def pipeline(eng, groups, ring, stages):
    def tick(t, h, has):
        for skew, f in stages:
            if has(skew):
                f(t - skew, (h - skew) % ring)

    ticks(eng, groups, ring, max(skew for skew, _ in stages), tick)


def past(j, n):
    return not isinstance(j, int) or j >= n


def filled(j, slot, ring, inc):
    return (j // ring + 1) * inc if isinstance(j, int) else (j - slot) * (inc // ring) + inc


class Chain:

    def __init__(self, eng, sem, per):
        self.eng, self.sem, self.per, self.n, self.j = eng, sem, per, 0, 0

    def group(self, j):
        assert self.n in (0, self.per), self.n
        self.j, self.n = j, 0

    def mark(self, ins):
        ins.then_inc(self.sem, 1)
        self.n += 1

    def link(self, ins):
        self.mark(ins)
        self.eng.wait_ge(self.sem, self.j * self.per + self.n)


def settle(eng, K):
    eng.sem_inc(K.passed, 1)


def registers(nc, eng, engine, table, k, n, top):
    return nc.values_load_multi_w_load_instructions(table[0:1, ds(k, n)], engines=(engine,), min_val=0, max_val=top,
                                                    skip_runtime_bounds_check_because="the schedule bounds its values")[1]


class Windows:

    def __init__(self, nc, eng, engine, K, steps, ring, skew):
        self.get = lambda k, n: registers(nc, eng, engine, K.reg_w, k, n, WINDOWS - 1)
        self.steps, self.ring, self.skew, self.held = steps, ring, skew, None

    def of(self, j, slot, lag=0):
        n, k = self.steps, j * self.steps - lag
        if isinstance(j, int):
            skip = max(-k, 0)
            return [None] * skip + list(self.get(k + skip, n - skip))
        q = (slot + self.skew) % self.ring
        if q == 0:
            self.held = self.get(k, n * self.ring)
        return self.held[q * n:(q + 1) * n]


class Phase:

    def __init__(self, nc, name):
        self.nc, self.name, self.ctx = nc, name, ExitStack()

    def __enter__(self):
        self.ctx.__enter__()
        return self

    def __exit__(self, *e):
        return self.ctx.__exit__(*e)

    def sb(self, name, shape, dt=F32):
        return self.ctx.enter_context(self.nc.sbuf_tensor(f"{self.name}_{name}", shape, dt))

    def ps(self, name, shape):
        n = 1
        for x in shape[1:]:
            n *= x
        t = self.ctx.enter_context(self.nc.psum_tensor(f"{self.name}_{name}", [shape[0], -(-n // 512) * 512], F32))
        if len(shape) == 2:
            return t[:, 0:n]
        dims = dict(zip("bcd", shape[2:]))
        names = " ".join("abcd"[:len(shape) - 1])
        return t[:, 0:n].rearrange(f"p ({names}) -> p {names}", **dims)

    def sem(self, name):
        return self.ctx.enter_context(self.nc.semaphore(f"{self.name}_{name}"))

    def block(self):
        return self.ctx.enter_context(self.nc.Block())


def constants(nc, K):
    with Phase(nc, "const") as ph:
        ramp_i = ph.sb("ramp_i", [P, 256], I32)
        part_i = ph.sb("part_i", [P, 1], I32)
        head_i = ph.sb("head_i", [P, 1], I32)
        grid_i = ph.sb("grid_i", [P, KC], I32)
        headf = ph.sb("headf", [P, 1])
        s_iota = ph.sem("iota")
        block = ph.block()

        @block.gpsimd
        def _(pool):
            pool.iota(ramp_i[:, :], [[1, 256]], base=0, channel_multiplier=0).then_inc(s_iota, 1)
            pool.iota(part_i[:, :], [[0, 1]], base=0, channel_multiplier=1).then_inc(s_iota, 1)
            pool.iota(grid_i[:, :], [[1, KC]], base=0, channel_multiplier=KC).then_inc(s_iota, 1)

        @block.vector
        def _(dve):
            dve.wait_ge(s_iota, 3)
            L = K.setup.on(dve)
            L.mark(dve.tensor_copy(K.ramp[:, :], ramp_i[:, :]))
            L.mark(dve.tensor_copy(K.part[:, :], part_i[:, :]))
            L.mark(dve.tensor_copy(K.grid[:, :], grid_i[:, :]))
            L.link(dve.tensor_scalar(head_i[:, :], part_i[:, :], 4, None, ALU.arith_shift_right))
            L.link(dve.tensor_copy(headf[:, :], head_i[:, :]))
            L.mark(dve.tensor_scalar(K.ident[:, :], K.ramp[:, 0:P], K.part[:, 0:1], None, ALU.is_equal))
            L.mark(dve.tensor_scalar(K.identb[:, :], K.ramp[:, 0:P], K.part[:, 0:1], None, ALU.is_equal))
            L.mark(dve.tensor_scalar(K.identb128[:, :], K.ramp[:, 0:P], K.part[:, 0:1], float(P), ALU.is_equal, ALU.mult))
            L.mark(dve.tensor_scalar(K.upto[:, :], K.ramp[:, 0:P], K.part[:, 0:1], None, ALU.is_le))
            L.mark(dve.tensor_scalar(K.headmask[:, :], K.ramp[:, 0:H], headf[:, 0:1], None, ALU.is_equal))
            L.mark(dve.tensor_scalar(K.trash[:, :], K.part[:, 0:1], float(NP), None, ALU.add))
            L.link(dve.memset(K.ones[:, :], 1.0))


def schedule(nc, K, T):
    with Phase(nc, "sched") as ph:
        first = ph.sb("first", [P, BLOCKS], I32)
        junk = ph.sb("junk", [P, BLOCKS])
        edge_of = ph.sb("edge_of", [P, 1])
        blocks = ph.sb("blocks", [P, 1])
        block_i = ph.sb("block_i", [P, 1], I32)
        blockf = ph.sb("blockf", [P, 1])
        dst = ph.sb("dst", [P, P], I32)
        within = ph.sb("within", [P, 1])
        offset = ph.sb("offset", [P, 1])
        diag = ph.sb("diag", [P, WINDOWS + 1])
        off = ph.sb("off", [P, WINDOWS + 1])
        count = ph.sb("count", [P, WINDOWS], I32)
        tiles_i = ph.sb("tiles_i", [P, WINDOWS], I32)
        tiles = ph.sb("tiles", [P, WINDOWS])
        start = ph.sb("start", [P, WINDOWS + 1])
        end = ph.sb("end", [P, WINDOWS])
        shift = ph.sb("shift", [P, WINDOWS + 1])
        cmp = ph.sb("cmp", [P, KC, WINDOWS])
        hot = ph.sb("hot", [P, KC, WINDOWS + 1])
        wk = ph.sb("wk", [P, KC])
        ek = ph.sb("ek", [P, KC])
        w_out = ph.sb("w_out", [P, KC], I32)
        e_out = ph.sb("e_out", [P, KC], I32)
        off_ps = ph.ps("off_ps", [P, WINDOWS + 1])
        s_first, s_blk, s_get, s_diag, s_pe, s_t, s_back = (
            ph.sem(x) for x in ("first", "blk", "get", "diag", "pe", "t", "back"))
        block = ph.block()

        @block.sync
        def _(sp):
            sp.dma_start(first[:, :], T.first.to_broadcast([P, BLOCKS])).then_inc(s_first, 16)
            sp.wait_ge(s_t, 1)
            sp.dma_start(T.sched_w.rearrange("(p c) -> p c", c=KC), w_out[:, :]).then_inc(s_first, 16)
            sp.dma_start(T.sched_e.rearrange("(p c) -> p c", c=KC), e_out[:, :]).then_inc(s_first, 16)
            sp.wait_ge(s_first, 48)
            settle(sp, K)
            sp.dma_start(K.reg_w[:, :], T.sched_w.rearrange("(a s) -> a s", a=1)).then_inc(s_back, 16)
            sp.dma_start(K.reg_e[:, :], T.sched_e.rearrange("(a s) -> a s", a=1)).then_inc(s_back, 16)
            sp.dma_start(K.wstep_i[:, :], T.sched_w.rearrange("(a s) -> a s", a=1)[:, 0:STEPS]
                         .to_broadcast([P, STEPS])).then_inc(s_back, 16)
            sp.wait_ge(s_back, 48)

        @block.tensor
        def _(pe):
            pe.wait_ge(s_diag, 1)
            pe.matmul(off_ps[:, :], K.ones[:, :], diag[:, :], start=True, stop=True).then_inc(s_pe, 1)

        @block.gpsimd
        def _(pool):
            pool.wait_ge(s_blk, 1)
            settle(pool, K)
            pool.indirect_dma_start(dst[:, :], None, T.dst,
                                    bass.IndirectOffsetOnAxis(ap=block_i[:, 0:1], axis=0)).then_inc(s_get, 16)

        @block.vector
        def _(dve):
            L = K.setup.on(dve)
            L.link(dve.tensor_scalar(edge_of[:, :], K.part[:, :], float(WIN), None, ALU.mult))
            dve.wait_ge(s_first, 16)
            L.link(dve.tensor_scalar(junk[:, :], first[:, :], edge_of[:, 0:1], 0.0, ALU.is_lt, ALU.add,
                                     accum_out=blocks[:, 0:1]))
            L.link(dve.tensor_scalar(blockf[:, :], blocks[:, :], 1.0, 0.0, ALU.subtract, ALU.max))
            dve.tensor_copy(block_i[:, :], blockf[:, :]).then_inc(s_blk, 1)
            dve.wait_ge(s_get, 16)
            L.link(dve.tensor_scalar(junk[:, 0:P], dst[:, :], edge_of[:, 0:1], 0.0, ALU.is_lt, ALU.add,
                                     accum_out=within[:, 0:1]))
            L.link(dve.scalar_tensor_tensor(offset[:, :], blockf[:, :], float(P), within[:, :], ALU.mult, ALU.add))
            dve.tensor_scalar(diag[:, :], K.ident[:, 0:WINDOWS + 1], offset[:, 0:1], None, ALU.mult).then_inc(s_diag, 1)
            dve.wait_ge(s_pe, 1)
            L.link(dve.tensor_copy(off[:, :], off_ps[:, :]))
            W = WINDOWS
            L.link(dve.tensor_tensor(count[:, :], off[:, 1:W + 1], off[:, 0:W], ALU.subtract))
            L.link(dve.tensor_scalar(count[:, :], count[:, :], float(P - 1), None, ALU.add))
            L.link(dve.tensor_scalar(tiles_i[:, :], count[:, :], 7, None, ALU.arith_shift_right))
            L.link(dve.tensor_copy(tiles[:, :], tiles_i[:, :]))
            L.link(dve.tensor_tensor_scan(end[:, :], K.ones[:, 0:W], tiles[:, :], 0.0, ALU.mult, ALU.add))
            L.mark(dve.tensor_tensor(start[:, 0:W], end[:, :], tiles[:, :], ALU.subtract))
            L.link(dve.tensor_copy(start[:, W:W + 1], end[:, W - 1:W]))
            L.link(dve.scalar_tensor_tensor(shift[:, :], start[:, :], -float(P), off[:, :], ALU.mult, ALU.add))
            L.link(dve.tensor_tensor(cmp[:, :, :], end[:, :].unsqueeze(1).to_broadcast([P, KC, W]),
                                     K.grid[:, :].unsqueeze(2).to_broadcast([P, KC, W]), ALU.is_le))
            L.link(dve.tensor_reduce(wk[:, :], cmp[:, :, :], AX.X, ALU.add))
            L.link(dve.tensor_tensor(hot[:, :, :], K.ramp[:, 0:W + 1].unsqueeze(1).to_broadcast([P, KC, W + 1]),
                                     wk[:, :].unsqueeze(2).to_broadcast([P, KC, W + 1]), ALU.is_equal))
            L.link(dve.tensor_tensor(hot[:, :, :], hot[:, :, :],
                                     shift[:, :].unsqueeze(1).to_broadcast([P, KC, W + 1]), ALU.mult))
            L.link(dve.tensor_reduce(ek[:, :], hot[:, :, :], AX.X, ALU.add))
            L.link(dve.scalar_tensor_tensor(ek[:, :], K.grid[:, :], float(P), ek[:, :], ALU.mult, ALU.add))
            L.link(dve.tensor_scalar(e_out[:, :], ek[:, :], float(N_EDGES), None, ALU.min))
            dve.tensor_scalar(w_out[:, :], wk[:, :], float(W - 1), None, ALU.min).then_inc(s_t, 1)
            dve.wait_ge(s_back, 48)
            L.link(dve.tensor_scalar(K.wbase[:, :], K.wstep_i[:, :], float(WIN), None, ALU.mult))



def node_inputs(nc, K, T):
    with Phase(nc, "node") as ph:
        NA = 2 * R + 2
        YW = R * H + C + 2 * H
        x = ph.sb("x", [P, TILES, C])
        squares = ph.sb("squares", [P, TILES, C])
        mean = ph.sb("mean", [P, TILES])
        rstd = ph.sb("rstd", [P, TILES])
        w_rel = ph.sb("w_rel", [P, R, C])
        w_y = ph.sb("w_y", [P, YW])
        w_ed = ph.sb("w_ed", [P, R, H])
        w_t = ph.sb("w_t", [P, R + 1, C])
        att = ph.sb("att", [P, NA])
        adiag = ph.sb("adiag", [P, NA, H])
        h = ph.sb("h", [P, 2, C])
        hT = ph.sb("hT", [P, 2, P])
        rows = ph.sb("rows", [P, 2, R, XR])
        srow = ph.sb("srow", [P, 2, C + 2 * H])
        hT_ps = [ph.ps(f"hT_ps{b}", [P, P]) for b in range(2)]
        x_ps = [ph.ps(f"x_ps{b}", [P, R, C]) for b in range(2)]
        y_ps = [ph.ps(f"y_ps{b}", [P, YW]) for b in range(2)]
        e_ps = [ph.ps(f"e_ps{b}", [WIN, 2, R * H]) for b in range(2)]
        s_w, s_x, s_v, s_adiag, s_fold, s_cent, s_sq, s_var, s_sd, s_norm = (
            ph.sem(n) for n in ("w", "x", "v", "adiag", "fold", "cent", "sq", "var", "sd", "norm"))
        s_h, s_hT, s_hTs, s_prod, s_rel, s_small = (ph.sem(n) for n in ("h", "hT", "hTs", "prod", "rel", "small"))
        s_st = [ph.sem(f"st{b}") for b in range(2)]
        block = ph.block()

        @block.sync
        def _(sp):
            sp.dma_start(x[:, :, :], T.x.rearrange("(t p) c -> p t c", p=P)).then_inc(s_x, 16)
            sp.dma_start(w_rel[:, :, :], T.W_rel.rearrange("r i o -> i r o")).then_inc(s_w, 16)
            sp.dma_start(w_y[:, R * H:R * H + C], T.W_self).then_inc(s_w, 16)
            sp.dma_start(w_t[:, 0:R, :], T.W_relT.rearrange("r o i -> o r i")).then_inc(s_w, 16)
            sp.dma_start(w_t[:, R, :], T.W_selfT).then_inc(s_w, 16)
            sp.dma_start(att[:, :], T.att).then_inc(s_w, 16)

            def store(t, b):
                sp.wait_ge(s_rel, t + 1)
                sp.wait_ge(s_small, t + 1)
                sp.dma_start(T.xrel.rearrange("(r n) c -> n r c", r=R)[ds(t * P, P), :, :],
                             rows[:, b, :, :]).then_inc(s_st[b], 16)
                sp.dma_start(T.esrc.rearrange("(r n) c -> n r c", r=R)[ds(t * P, P), :, :],
                             rows[:, b, :, C:XR]).then_inc(s_st[b], 16)
                sp.dma_start(T.srow[ds(t * P, P), :], srow[:, b, :]).then_inc(s_st[b], 16)

            pipeline(sp, TILES, 2, [(0, store)])
            for b in range(2):
                sp.wait_ge(s_st[b], 48 * (TILES // 2))

        @block.vector
        def _(dve):
            L, M = Links(dve, s_v), K.setup.on(dve)
            dve.wait_ge(s_w, 80)
            dve.tensor_tensor(adiag[:, :, :], att[:, :].unsqueeze(2).to_broadcast([P, NA, H]),
                              K.headmask[:, :].unsqueeze(1).to_broadcast([P, NA, H]), ALU.mult).then_inc(s_adiag, 1)
            dve.wait_ge(s_fold, 1)
            f = x_ps[0][:, 0, 0:2 * R * H].rearrange("p (r s h) -> p r s h", r=R, s=2)
            L.mark(dve.tensor_copy(w_y[:, 0:R * H].rearrange("p (r h) -> p r h", r=R), f[:, :, 0, :]))
            L.mark(dve.tensor_copy(w_ed[:, :, :], f[:, :, 1, :]))
            L.mark(dve.tensor_copy(w_y[:, R * H + C:YW], y_ps[0][:, 0:2 * H]))
            dve.wait_ge(s_x, 16)
            M.link(dve.tensor_reduce(mean[:, :], x[:, :, :], AX.X, ALU.add))
            M.link(dve.tensor_scalar(mean[:, :], mean[:, :], 1.0 / C, None, ALU.mult))
            for q in range(2):
                half = slice(q * TILES // 2, (q + 1) * TILES // 2)
                dve.tensor_tensor(x[:, half, :], x[:, half, :],
                                  mean[:, half].unsqueeze(2).to_broadcast([P, TILES // 2, C]), ALU.subtract).then_inc(s_cent, 1)
            for q in range(2):
                half = slice(q * TILES // 2, (q + 1) * TILES // 2)
                dve.wait_ge(s_sq, q + 1)
                M.mark(dve.tensor_reduce(rstd[:, half], squares[:, half, :], AX.X, ALU.add))
            M.wait()
            dve.tensor_scalar(rstd[:, :], rstd[:, :], 1.0 / C, EPS, ALU.mult, ALU.add).then_inc(s_var, 1)
            dve.wait_ge(s_sd, 1)
            dve.reciprocal(rstd[:, :], rstd[:, :]).then_inc(s_norm, 1)

            def evacuate(t, b):
                dve.wait_ge(s_hT, t + 1)
                if past(t, 2):
                    dve.wait_ge(s_prod, t - 1)
                dve.tensor_copy(hT[:, b, :], hT_ps[b][:, :]).then_inc(s_hTs, 1)

            def rest(t, b):
                dve.wait_ge(s_prod, t + 1)
                if past(t, 2):
                    dve.wait_ge(s_st[b], (t - b) * 24)
                dve.tensor_copy(rows[:, b, :, C:XR], y_ps[b][:, 0:R * H].rearrange("p (r h) -> p r h", r=R))
                dve.tensor_copy(srow[:, b, :], y_ps[b][:, R * H:YW])
                dve.tensor_copy(K.ed[:, ds(t * 2, 2), :], e_ps[b][:, :, :]).then_inc(s_small, 1)

            pipeline(dve, TILES, 2, [(0, evacuate), (1, rest)])

        @block.scalar
        def _(act):
            for q in range(2):
                half = slice(q * TILES // 2, (q + 1) * TILES // 2)
                act.wait_ge(s_cent, q + 1)
                act.activation(squares[:, half, :], x[:, half, :], ACT.Square).then_inc(s_sq, 1)
            act.wait_ge(s_var, 1)
            act.activation(rstd[:, :], rstd[:, :], ACT.Sqrt).then_inc(s_sd, 1)
            act.wait_ge(s_norm, 1)

            def normalize(t, b):
                if past(t, 2):
                    act.wait_ge(s_hT, t - 1)
                act.activation(h[:, b, :], x[:, ds(t, 1), :].rearrange("p a c -> p (a c)"), ACT.Relu,
                               scale=rstd[:, ds(t, 1)]).then_inc(s_h, 1)

            def evacuate(t, b):
                act.wait_ge(s_prod, t + 1)
                if past(t, 2):
                    act.wait_ge(s_st[b], (t - b) * 24)
                act.activation(rows[:, b, :, 0:C], x_ps[b][:, :, :], ACT.Copy).then_inc(s_rel, 1)

            pipeline(act, TILES, 2, [(0, normalize), (2, evacuate)])

        @block.tensor
        def _(pe):
            pe.wait_ge(s_w, 80)
            pe.wait_ge(s_adiag, 1)
            for r in range(R):
                pe.matmul(x_ps[0][:, 0, r * 2 * H:(r + 1) * 2 * H], w_t[:, r, :],
                          flat(adiag[:, 2 * r:2 * r + 2, :]), start=True, stop=True)
            pe.matmul(y_ps[0][:, 0:2 * H], w_t[:, R, :], flat(adiag[:, 2 * R:NA, :]),
                      start=True, stop=True).then_inc(s_fold, 1)
            pe.wait_ge(s_v, 3)

            def transpose(t, b):
                pe.wait_ge(s_h, t + 1)
                if past(t, 2):
                    pe.wait_ge(s_hTs, t - 1)
                pe.transpose(hT_ps[b][:, :], h[:, b, :], K.ident[:, :]).then_inc(s_hT, 1)

            def products(t, b):
                pe.wait_ge(s_hTs, t + 1)
                if past(t, 2):
                    pe.wait_ge(s_rel, t - 1)
                    pe.wait_ge(s_small, t - 1)
                pe.matmul(flat(x_ps[b][:, :, :]), hT[:, b, :], flat(w_rel[:, :, :]), start=True, stop=True)
                pe.matmul(y_ps[b][:, :], hT[:, b, :], w_y[:, :], start=True, stop=True)
                for q in range(2):
                    last = pe.matmul(e_ps[b][:, q, :], hT[:, b, q * WIN:(q + 1) * WIN], flat(w_ed[:, :, :]),
                                     start=True, stop=True)
                last.then_inc(s_prod, 1)

            pipeline(pe, TILES, 2, [(0, transpose), (1, products)])


def relation_maxima(nc, K, T):
    with Phase(nc, "max") as ph:
        GROUPS = STEPS // G
        rec = ph.sb("rec", [P, 2, G, REC], I32)
        idx = ph.sb("idx", [P, 2, G], I32)
        isnext = ph.sb("isnext", [P, 2, G])
        isprev = ph.sb("isprev", [P, 2, G])
        lastloc = ph.sb("lastloc", [P, 2, G])
        begins = ph.sb("begins", [P, STEPS], BF16)
        mask = ph.sb("mask", [P, 2, G, R])
        outside = ph.sb("outside", [P, 2, G, R])
        es = ph.sb("es", [P, 4, G, H])
        beg = ph.sb("beg", [P, 2, G], BF16)
        m = ph.sb("m", [P, 2, G, R * H])
        mT = ph.sb("mT", [R * H, 2, G * P])
        run = ph.sb("run", [R * H, 2, G * P])
        runT = ph.sb("runT", [P, 2, G, R * H + 1])
        onehot = ph.sb("onehot", [P, 4, G, WIN])
        maxima = ph.sb("maxima", [WIN, WSLOTS, R * H + 1])
        mm = ph.sb("mm", [WIN, WSLOTS, R, H])
        both = ph.sb("both", [WIN, WSLOTS, R, 2, H])
        valid = ph.sb("valid", [WIN, WSLOTS, R])
        none = ph.sb("none", [WIN, WSLOTS])
        mT_ps = ph.ps("mT_ps", [R * H, G * P])
        beg_ps = ph.ps("beg_ps", [R * H, G * P])
        runT_ps = ph.ps("runT_ps", [P, G, R * H])
        node_ps = [ph.ps(f"node_ps{b}", [WIN, G, R * H + 1]) for b in range(2)]
        s_rec = [ph.sem(f"rec{b}") for b in range(2)]
        s_es = [ph.sem(f"es{b}") for b in range(4)]
        s_pc, s_prep, s_mc, s_m, s_tr, s_mt, s_scan, s_bk, s_rt, s_oh, s_node, s_acc = (
            ph.sem(n) for n in ("pc", "prep", "mc", "m", "tr", "mt", "scan", "bk", "rt", "oh", "node", "acc"))
        s_init, s_fin, s_out = (ph.sem(n) for n in ("init", "fin", "out"))
        block = ph.block()

        @block.sync
        def _(sp):
            def load(j, b):
                e = registers(nc, sp, mybir.EngineType.SP, K.reg_e, j * G, G, N_EDGES)
                if past(j, 2):
                    sp.wait_ge(s_prep, j - 1)
                for u in range(G):
                    sp.dma_start(rec[:, b, u, :], T.rec[ds(e[u], P), :]).then_inc(s_rec[b], 16)

            pipeline(sp, GROUPS, 2, [(0, load)])
            sp.wait_ge(s_fin, 1)
            sp.dma_start(T.edm.rearrange("(w n) c -> n w c", n=WIN),
                         both[:, :, :, :, :].rearrange("n w r s h -> n w (r s h)")).then_inc(s_out, 16)
            sp.dma_start(T.valid.rearrange("(w n) r -> n w r", n=WIN), valid[:, :, :]).then_inc(s_out, 16)
            sp.wait_ge(s_out, 32)

        @block.gpsimd
        def _(pool):
            def gather(j, b):
                pool.wait_ge(s_prep, j + 1)
                if past(j, 4):
                    pool.wait_ge(s_m, j - 3)
                settle(pool, K)
                for u in range(G):
                    pool.indirect_dma_start(es[:, b, u, :], None, T.esrc,
                                            bass.IndirectOffsetOnAxis(ap=idx[:, b % 2, u:u + 1], axis=0)).then_inc(s_es[b], 16)

            pipeline(pool, GROUPS, 4, [(0, gather)])

        @block.vector
        def _(dve):
            dve.memset(maxima[:, :, :], 0.0).then_inc(s_init, 1)
            dve.memset(runT[:, :, :, R * H:], 1.0).then_inc(s_init, 1)
            dve.wait_ge(s_init, 2)
            pc, mc = Chain(dve, s_pc, 12), Chain(dve, s_mc, 2)
            rel4 = K.ramp[:, 0:R].unsqueeze(1).to_broadcast([P, G, R])

            windows = Windows(nc, dve, mybir.EngineType.DVE, K, G, 4, 5)

            def prepare(j, slot, between):
                k, b = j * G, slot % 2
                src, dst, typ, prev, nxt = (rec[:, b, :, c] for c in range(5))
                dve.wait_ge(s_rec[b], filled(j, b, 2, 16 * G) if isinstance(j, int) else (j - b) * 8 * G + 16 * G)
                pc.group(j)
                loc, key = K.loc[:, ds(k, G)], K.key[:, ds(k, G)]
                pc.mark(dve.tensor_tensor(isnext[:, b, :], dst, nxt, ALU.not_equal))
                between(0)
                pc.mark(dve.tensor_tensor(isprev[:, b, :], dst, prev, ALU.not_equal))
                pc.mark(dve.tensor_tensor(loc, dst, K.wbase[:, ds(k, G)], ALU.subtract))
                pc.mark(dve.tensor_tensor(mask[:, b, :, :], rel4, typ.unsqueeze(2).to_broadcast([P, G, R]), ALU.is_equal))
                between(1)
                pc.mark(dve.scalar_tensor_tensor(idx[:, b, :], typ, float(NP), src, ALU.mult, ALU.add))
                pc.mark(dve.scalar_tensor_tensor(K.idx[:, ds(k, G)], typ, float(NP), src, ALU.mult, ALU.add))
                between(2)
                pc.mark(dve.tensor_copy(K.src[:, ds(k, G)], src))
                pc.mark(dve.tensor_copy(K.typ[:, ds(k, G)], typ))
                between(3)
                dve.wait_ge(s_pc, j * 12 + 8)
                pc.mark(dve.scalar_tensor_tensor(key, loc, float(R), typ, ALU.mult, ALU.add))
                pc.mark(dve.tensor_scalar(outside[:, b, :, :], mask[:, b, :, :], 1.0, BIG, ALU.subtract, ALU.mult))
                between(4)
                pc.mark(dve.tensor_scalar(begins[:, ds(k, G)], isprev[:, b, :], -BIG, None, ALU.mult))
                pc.mark(dve.scalar_tensor_tensor(lastloc[:, b, :], loc, 1.0, isnext[:, b, :], ALU.add, ALU.mult))
                between(5)
                between(6)
                dve.wait_ge(s_pc, j * 12 + 12)
                dve.tensor_scalar(lastloc[:, b, :], lastloc[:, b, :], 1.0, None, ALU.subtract).then_inc(s_prep, 1)
                between(7)

            def separate(j, slot):
                b = slot % 2
                dve.wait_ge(s_es[slot], filled(j, slot, 4, 16 * G))
                dve.wait_ge(s_prep, j + 1)
                if past(j, 2):
                    dve.wait_ge(s_tr, j - 1)
                mc.group(j)
                m4 = m[:, b, :, :].rearrange("p g (r h) -> p g r h", r=R)
                mc.mark(dve.tensor_tensor(m4, es[:, slot, :, :].unsqueeze(2).to_broadcast([P, G, R, H]),
                                          mask[:, b, :, :].unsqueeze(3).to_broadcast([P, G, R, H]), ALU.mult))
                mc.mark(dve.tensor_copy(beg[:, b, :], begins[:, ds(j * G, G)]))
                if past(j, 4):
                    dve.wait_ge(s_node, j - 3)
                dve.tensor_tensor(onehot[:, slot, :, :], K.ramp[:, 0:WIN].unsqueeze(1).to_broadcast([P, G, WIN]),
                                  lastloc[:, b, :].unsqueeze(2).to_broadcast([P, G, WIN]), ALU.is_equal).then_inc(s_oh, 1)
                dve.wait_ge(s_mc, j * 2 + 2)
                dve.tensor_tensor(m4, m4, outside[:, b, :, :].unsqueeze(3).to_broadcast([P, G, R, H]), ALU.add).then_inc(s_m, 1)

            def scan(j, slot):
                b = slot % 2
                dve.wait_ge(s_mt, j + 1)
                if past(j, 1):
                    dve.wait_ge(s_scan, j)
                if past(j, 2):
                    dve.wait_ge(s_bk, j - 1)
                first = isinstance(j, int) and j == 0
                dve.tensor_tensor_scan(run[:, b, :], beg_ps[:, :], mT[:, b, :],
                                       -BIG if first else run[:, 1 - b, G * P - 1:G * P],
                                       ALU.add, ALU.max).then_inc(s_scan, 1)

            def keep(j, slot, u, w):
                if u == 0:
                    dve.wait_ge(s_node, j + 1)
                if u or past(j, 1):
                    dve.wait_ge(s_acc, j * G + u)
                dst = maxima[:, ds(w, 1), :].rearrange("n a c -> n (a c)")
                dve.tensor_tensor(dst, dst, node_ps[slot % 2][:, u, :], ALU.add).then_inc(s_acc, 1)

            def tick(t, h, has):
                slot = lambda skew: (h - skew) % 4
                if has(5):
                    w = windows.of(t - 5, slot(5))
                if has(4):
                    scan(t - 4, slot(4))
                if has(2):
                    separate(t - 2, slot(2))
                between = lambda u: keep(t - 5, slot(5), u, w[u]) if has(5) else None
                if has(0):
                    prepare(t, h, between)
                else:
                    for u in range(G):
                        between(u)

            ticks(dve, GROUPS, 4, 5, tick)
            L = K.setup.on(dve)
            dve.wait_ge(s_acc, STEPS)
            ed4 = K.ed[:, :, :].rearrange("n w (r h) -> n w r h", r=R)
            mx = maxima[:, :, 0:R * H].rearrange("n w (r h) -> n w r h", r=R)
            wr = "n w r h -> n (w r) h"
            L.link(dve.tensor_scalar(none[:, :], maxima[:, :, R * H], 1.0, BIG, ALU.subtract, ALU.mult))
            L.link(dve.tensor_tensor(mm[:, :, :, :], mx, none[:, :].unsqueeze(2).unsqueeze(3)
                                     .to_broadcast([WIN, WSLOTS, R, H]), ALU.add))
            L.link(dve.tensor_scalar(valid[:, :, :], mm[:, :, :, 0], -0.9 * BIG, None, ALU.is_gt))
            L.link(dve.tensor_tensor(mm[:, :, :, :], mm[:, :, :, :], ed4, ALU.add))
            bv = both[:, :, :, :, :].rearrange("n w r s h -> n (w r) s h")
            L.mark(dve.scalar_tensor_tensor(bv[:, :, 1, :], mm[:, :, :, :].rearrange(wr), SLOPE0,
                                            mm[:, :, :, :].rearrange(wr), ALU.mult, ALU.max))
            L.link(dve.tensor_copy(bv[:, :, 0, :], ed4.rearrange(wr)))
            dve.sem_inc(s_fin, 1)

        @block.scalar
        def _(act):
            def move(j, b):
                act.wait_ge(s_tr, j + 1)
                if past(j, 2):
                    act.wait_ge(s_scan, j - 1)
                act.activation(mT[:, b, :], mT_ps[:, :], ACT.Copy).then_inc(s_mt, 1)

            def move_back(j, b):
                act.wait_ge(s_bk, j + 1)
                if past(j, 2):
                    act.wait_ge(s_node, j - 1)
                act.activation(runT[:, b, :, 0:R * H], runT_ps[:, :, :], ACT.Copy).then_inc(s_rt, 1)

            act.wait_ge(s_init, 2)
            pipeline(act, GROUPS, 2, [(1, move_back), (0, move)])

        @block.tensor
        def _(pe):
            def transpose(j, b):
                pe.wait_ge(s_m, j + 1)
                if past(j, 1):
                    pe.wait_ge(s_mt, j)
                    pe.wait_ge(s_scan, j)
                settle(pe, K)
                for u in range(G):
                    pe.transpose(mT_ps[:, u * P:(u + 1) * P], m[:, b % 2, u, :], K.ident[:, :])
                for u in range(G):
                    last = pe.matmul(beg_ps[:, u * P:(u + 1) * P], beg[:, b % 2, u:u + 1].to_broadcast([P, R * H]),
                                     K.identb[:, :], start=True, stop=True)
                last.then_inc(s_tr, 1)

            def back(j, b):
                pe.wait_ge(s_scan, j + 1)
                if past(j, 1):
                    pe.wait_ge(s_rt, j)
                settle(pe, K)
                for u in range(G):
                    last = pe.transpose(runT_ps[:, u, :], run[:, b % 2, u * P:(u + 1) * P], K.ident[0:R * H, 0:R * H])
                last.then_inc(s_bk, 1)

            def by_node(j, b):
                pe.wait_ge(s_rt, j + 1)
                pe.wait_ge(s_oh, j + 1)
                if past(j, 2):
                    pe.wait_ge(s_acc, (j - 1) * G)
                for u in range(G):
                    last = pe.matmul(node_ps[b % 2][:, u, :], onehot[:, b, u, :], runT[:, b % 2, u, :], start=True, stop=True)
                last.then_inc(s_node, 1)

            pe.wait_ge(s_init, 2)
            pipeline(pe, GROUPS, 4, [(1, back), (0, transpose), (1, by_node)])


def relation_attention(nc, K, T, acc):
    with Phase(nc, "att") as ph:
        U, RG = 4, 4
        DVE_HOTS = 2
        GROUPS = STEPS // U
        S2 = 2 * H
        idx = ph.sb("idx", [P, RG, U], I32)
        xg = ph.sb("xg", [P, RG, U, XR])
        onehot = ph.sb("onehot", [P, RG, U, WIN])
        onehotT = ph.sb("onehotT", [WIN, RG, U * P])
        edw = ph.sb("edw", [WIN, RG, U, R * S2])
        mask = ph.sb("mask", [P, RG, U, R])
        masked = ph.sb("masked", [P, U, R, S2])
        dstv = ph.sb("dstv", [P, U, S2])
        logit = ph.sb("logit", [P, U, H])
        leaky = ph.sb("leaky", [P, U, H])
        arg = ph.sb("arg", [P, RG, U, H])
        p = ph.sb("p", [P, RG, U, H])
        px = ph.sb("px", [P, RG, U, XR])
        keyhot = ph.sb("keyhot", [P, RG, U, R * WIN])
        away = ph.sb("away", [P, U - DVE_HOTS, R * WIN])
        oT_ps = ph.ps("oT_ps", [WIN, U * P])
        dst_ps = [ph.ps(f"dst_ps{b}", [P, U, R * S2]) for b in range(2)]
        sum_ps = [ph.ps(f"sum_ps{u}", [P, 2, XR]) for u in range(U)]
        s_xg = [ph.sem(f"xg{b}") for b in range(RG)]
        s_ed = [ph.sem(f"ed{b}") for b in range(RG)]
        s_idx, s_oh, s_tr, s_oT, s_dst, s_sc, s_sel, s_p, s_pc, s_px, s_kh, s_kha, s_away, s_sum, s_acc = (
            ph.sem(n) for n in ("idx", "oh", "tr", "oT", "dst", "sc", "sel", "p", "pc", "px", "kh", "kha", "away", "sum", "acc"))
        block = ph.block()

        @block.sync
        def _(sp):
            def load(j, b):
                w = registers(nc, sp, mybir.EngineType.SP, K.reg_w, j * U, U, WINDOWS - 1)
                if past(j, RG):
                    sp.wait_ge(s_dst, j - RG + 1)
                    settle(sp, K)
                for u in range(U):
                    sp.dma_start(edw[:, b, u, :], T.edm[ds(w[u] * WIN, WIN), :]).then_inc(s_ed[b], 16)

            pipeline(sp, GROUPS, RG, [(0, load)])

        @block.gpsimd
        def _(pool):
            def gather(j, b):
                pool.wait_ge(s_idx, j + 1)
                if past(j, RG):
                    pool.wait_ge(s_px, j - RG + 1)
                settle(pool, K)
                for u in range(U):
                    pool.indirect_dma_start(xg[:, b, u, :], None, T.xrel,
                                            bass.IndirectOffsetOnAxis(ap=idx[:, b, u:u + 1], axis=0)).then_inc(s_xg[b], 16)

            pipeline(pool, GROUPS, RG, [(0, gather)])

        @block.vector
        def _(dve):

            windows = Windows(nc, dve, mybir.EngineType.DVE, K, U, RG, 5)

            def hots(j, b):
                if past(j, RG):
                    dve.wait_ge(s_tr, j - RG + 1)
                dve.tensor_tensor(mask[:, b, :, :], K.ramp[:, 0:R].unsqueeze(1).to_broadcast([P, U, R]),
                                  K.typ[:, ds(j * U, U)].unsqueeze(2).to_broadcast([P, U, R]), ALU.is_equal)
                dve.tensor_tensor(onehot[:, b, :, :], K.ramp[:, 0:WIN].unsqueeze(1).to_broadcast([P, U, WIN]),
                                  K.loc[:, ds(j * U, U)].unsqueeze(2).to_broadcast([P, U, WIN]), ALU.is_equal).then_inc(s_oh, 1)

            def keyhots(j, b, u):
                if past(j, RG) and u == 0:
                    dve.wait_ge(s_sum, (j - RG + 1) * U)
                dve.tensor_scalar(keyhot[:, b, u, :], K.ramp[:, :], K.key[:, ds(j * U + u, 1)], None,
                                  ALU.is_equal).then_inc(s_kh, 1)

            def select(j, b, step):
                if step == 0:
                    dve.wait_ge(s_dst, j + 1)
                    dve.wait_ge(s_oh, j + 1)
                    ins = dve.tensor_tensor(masked[:, :, :, :], dst_ps[b % 2][:, :, :].rearrange("p u (r c) -> p u r c", r=R),
                                            mask[:, b, :, :].unsqueeze(3).to_broadcast([P, U, R, S2]), ALU.mult)
                    ins.then_inc(s_sc, 1)
                    return
                dve.wait_ge(s_sc, j * 4 + step)
                if step == 1:
                    ins = dve.tensor_reduce(dstv[:, :, :], masked[:, :, :, :].rearrange("p u r c -> p u c r"), AX.X, ALU.add)
                elif step == 2:
                    dve.wait_ge(s_xg[b], filled(j, b, RG, 16 * U))
                    ins = dve.tensor_tensor(logit[:, :, :], xg[:, b, :, C:XR], dstv[:, :, 0:H], ALU.add)
                elif step == 3:
                    ins = dve.scalar_tensor_tensor(leaky[:, :, :], logit[:, :, :], SLOPE0, logit[:, :, :], ALU.mult, ALU.max)
                else:
                    if past(j, RG):
                        dve.wait_ge(s_p, j - RG + 1)
                    dve.tensor_tensor(arg[:, b, :, :], leaky[:, :, :], dstv[:, :, H:S2], ALU.subtract).then_inc(s_sel, 1)
                    return
                ins.then_inc(s_sc, 1)

            def bound(j, b):
                dve.wait_ge(s_p, j + 1)
                if past(j, RG):
                    dve.wait_ge(s_sum, (j - RG + 1) * U)
                dve.tensor_scalar(px[:, b, :, C:XR], p[:, b, :, :], 1.0, None, ALU.min).then_inc(s_pc, 1)

            def weigh(j, b):
                dve.wait_ge(s_pc, j + 1)
                dve.tensor_tensor(px[:, b, :, 0:C].rearrange("p u (h d) -> p u h d", h=H),
                                  xg[:, b, :, 0:C].rearrange("p u (h d) -> p u h d", h=H),
                                  px[:, b, :, C:XR].unsqueeze(3).to_broadcast([P, U, H, D]), ALU.mult).then_inc(s_px, 1)

            def add(j, b, u, w):
                dve.wait_ge(s_sum, j * U + u + 1)
                dve.wait_ge(s_acc, j * U + u + 1)
                dst = acc[:, ds(w, 1), :, :].rearrange("n a b c -> n (a b c)")
                dve.tensor_tensor(dst, dst, flat(sum_ps[u][:, :, :]), ALU.add).then_inc(s_acc, 1)

            def tick(t, h, has):
                slot = lambda skew: (h - skew) % RG
                if has(5):
                    w = windows.of(t - 5, slot(5))
                if has(0):
                    hots(t, h)
                if isinstance(t, int) and t == 4:
                    dve.memset(acc[:, :, :, :], 0.0).then_inc(s_acc, 1)
                if has(4):
                    bound(t - 4, slot(4))
                if has(3):
                    select(t - 3, slot(3), 0)
                if has(4):
                    weigh(t - 4, slot(4))
                for u in range(U):
                    if has(5):
                        add(t - 5, slot(5), u, w[u])
                    if has(3):
                        select(t - 3, slot(3), u + 1)
                        if u < DVE_HOTS:
                            keyhots(t - 3, slot(3), u)

            ticks(dve, GROUPS, RG, 5, tick)
            dve.wait_ge(s_acc, STEPS + 1)

        @block.scalar
        def _(act):
            def indices(j, b):
                if past(j, RG):
                    act.wait_ge(s_xg[b], filled(j, b, RG, 16 * U) - 16 * U)
                act.activation(idx[:, b, :], K.idx[:, ds(j * U, U)], ACT.Copy).then_inc(s_idx, 1)

            def move(j, b):
                act.wait_ge(s_tr, j + 1)
                if past(j, RG):
                    act.wait_ge(s_dst, j - RG + 1)
                act.activation(onehotT[:, b, :], oT_ps[:, :], ACT.Copy).then_inc(s_oT, 1)

            def exponentials(j, b):
                act.wait_ge(s_sel, j + 1)
                if past(j, RG):
                    act.wait_ge(s_px, j - RG + 1)
                act.activation(p[:, b, :, :], arg[:, b, :, :], ACT.Exp).then_inc(s_p, 1)

            away_chain = Chain(act, s_away, U - DVE_HOTS)

            def keyhots(j, b):
                if past(j, RG):
                    act.wait_ge(s_sum, (j - RG + 1) * U)
                if past(j, 1):
                    act.wait_ge(s_kha, j)
                away_chain.group(j)
                for q in range(U - DVE_HOTS):
                    away_chain.mark(act.activation(away[:, q, :], K.ramp[:, :], ACT.Abs,
                                                   bias=K.key[:, ds(j * U + DVE_HOTS + q, 1)], scale=-1.0))
                act.wait_ge(s_away, (j + 1) * (U - DVE_HOTS))
                act.activation(keyhot[:, b, DVE_HOTS:U, :], away[:, :, :], ACT.Relu, bias=K.ones[:, 0:1],
                               scale=-1.0).then_inc(s_kha, 1)

            pipeline(act, GROUPS, RG, [(4, exponentials), (0, indices), (1, move), (3, keyhots)])

        @block.tensor
        def _(pe):
            def transpose(j, b):
                pe.wait_ge(s_oh, j + 1)
                if past(j, 1):
                    pe.wait_ge(s_oT, j)
                settle(pe, K)
                for u in range(U):
                    last = pe.transpose(oT_ps[:, u * P:(u + 1) * P], onehot[:, b, u, :], K.ident[:, :])
                last.then_inc(s_tr, 1)

            def expand(j, b):
                pe.wait_ge(s_oT, j + 1)
                pe.wait_ge(s_ed[b], filled(j, b, RG, 16 * U))
                if past(j, 2):
                    pe.wait_ge(s_sel, j - 1)
                for u in range(U):
                    last = pe.matmul(dst_ps[b % 2][:, u, :], onehotT[:, b, u * P:(u + 1) * P], edw[:, b, u, :],
                                     start=True, stop=True)
                last.then_inc(s_dst, 1)

            def sums(j, b):
                pe.wait_ge(s_kh, (j + 1) * DVE_HOTS)
                pe.wait_ge(s_kha, j + 1)
                pe.wait_ge(s_px, j + 1)
                for u in range(U):
                    if past(j, 1):
                        pe.wait_ge(s_acc, (j - 1) * U + u + 2)
                    for q in range(2):
                        last = pe.matmul(sum_ps[u][:, q, :], keyhot[:, b, u, q * P:(q + 1) * P], px[:, b, u, :],
                                         start=True, stop=True)
                    last.then_inc(s_sum, 1)

            pipeline(pe, GROUPS, RG, [(4, sums), (1, expand), (0, transpose)])


def node_update(nc, K, T, acc):
    with Phase(nc, "upd") as ph:
        CH = 4
        HALVES = WSLOTS * 2
        acc_h = acc[:, :, :, :].rearrange("p w q c -> p (w q) c")
        bias = ph.sb("bias", [P, C])
        RT = 4
        zero = ph.sb("zero", [P, 4 * HID])
        rden = ph.sb("rden", [P, RT, CH, H])
        tmp = ph.sb("tmp", [P, RT, CH, C])
        s_b, s_c, s_n, s_g, s_gd, s_z, s_zd = (ph.sem(n) for n in ("b", "c", "n", "g", "gd", "z", "zd"))
        block = ph.block()

        @block.sync
        def _(sp):
            sp.dma_start(bias[:, :], T.bias_rel.unsqueeze(0).to_broadcast([P // R, R, C])).then_inc(s_b, 16)
            sp.wait_ge(s_z, 1)
            for tab in T.sums:
                rows = tab.rearrange("(a p f) c -> a p (f c)", p=P, f=4)
                for a in range(rows.shape[0]):
                    sp.dma_start(rows[a, :, :], zero[:, :]).then_inc(s_zd, 16)
            sp.wait_ge(s_zd, 16 * 2 * rows.shape[0])

        @block.vector
        def _(dve):
            c = Chain(dve, s_c, 2)

            def normalize(j, b):
                c.group(j)
                if past(j, RT):
                    dve.wait_ge(s_gd, j - RT + 1)
                part = acc_h[:, ds(j * CH, CH), :]
                c.link(dve.tensor_scalar(rden[:, b, :, :], part[:, :, C:XR], 1e-30, None, ALU.max))
                c.link(dve.reciprocal(rden[:, b, :, :], rden[:, b, :, :]))
                dve.tensor_tensor(tmp[:, b, :, :].rearrange("p k (h d) -> p k h d", h=H),
                                  part[:, :, 0:C].rearrange("p k (h d) -> p k h d", h=H),
                                  rden[:, b, :, :].unsqueeze(3).to_broadcast([P, CH, H, D]), ALU.mult).then_inc(s_n, 1)

            pipeline(dve, HALVES // CH, RT, [(0, normalize)])

        @block.gpsimd
        def _(pool):
            pool.memset(zero[:, :], 0.0).then_inc(s_z, 1)
            pool.wait_ge(s_b, 16)

            def add_bias(j, b):
                pool.wait_ge(s_n, j + 1)
                pool.tensor_tensor(tmp[:, b, :, :], tmp[:, b, :, :],
                                   bias[:, :].unsqueeze(1).to_broadcast([P, CH, C]), ALU.add).then_inc(s_g, 1)

            pipeline(pool, HALVES // CH, RT, [(0, add_bias)])

        @block.scalar
        def _(act):
            def gelu(j, b):
                act.wait_ge(s_g, j + 1)
                act.activation(acc_h[:, ds(j * CH, CH), 0:C], tmp[:, b, :, :], ACT.Gelu).then_inc(s_gd, 1)

            pipeline(act, HALVES // CH, RT, [(0, gelu)])
            act.wait_ge(s_gd, HALVES // CH)

    with Phase(nc, "mix") as ph:
        M = R + 1
        RG = 4
        CR = C + H
        x = ph.sb("x", [P, RG, C])
        xb = ph.sb("xb", [P, RG, C])
        ld = ph.sb("ld", [P, RG, H])
        w_c = ph.sb("w_c", [P, CR])
        w_cT = ph.sb("w_cT", [P, C])
        att = ph.sb("att", [P, 2 * R + 2])
        adiag = ph.sb("adiag", [P, H])
        blang = ph.sb("blang", [P, C])
        valid = ph.sb("valid", [P, TILES, R])
        hide = ph.sb("hide", [P, TILES, R])
        g = ph.sb("g", [P, 2, 4, C])
        gT = ph.sb("gT", [P, 2, 4 * P])
        ent = ph.sb("ent", [P, RG, M, C])
        ls = ph.sb("ls", [P, RG, M, H])
        t1 = ph.sb("t1", [P, M, H])
        top = ph.sb("top", [P, H])
        al = ph.sb("al", [P, 2, M, H])
        ex = ph.sb("ex", [P, 2, M, H])
        den = ph.sb("den", [P, H])
        prod = ph.sb("prod", [P, M, C])
        mixed = ph.sb("mixed", [P, C])
        out = ph.sb("out", [P, 2, C])
        stats = ph.sb("stats", [P, 6])
        mv = ph.sb("mv", [P, 2])
        gT_ps = [ph.ps(f"gT_ps{b}", [P, 4 * P]) for b in range(2)]
        h_ps = [[ph.ps(f"h_ps{b}{q}", [P, 2, CR]) for q in range(2)] for b in range(2)]
        f_ps = ph.ps("f_ps", [P, H])
        s_w, s_adiag, s_fold, s_wc, s_gT, s_gTs, s_h, s_ent, s_c, s_arg, s_ex, s_out, s_gend = (
            ph.sem(n) for n in ("w", "adiag", "fold", "wc", "gT", "gTs", "h", "ent", "c", "arg", "ex", "out", "gend"))
        s_g, s_xb, s_stat = ph.sem("g"), ph.sem("xb"), ph.sem("stat")
        s_in = [ph.sem(f"in{b}") for b in range(RG)]
        s_st = [ph.sem(f"st{b}") for b in range(2)]
        block = ph.block()

        @block.gpsimd
        def _(pool):
            def take(t, b):
                if past(t, 2):
                    pool.wait_ge(s_gT, t - 1)
                pool.tensor_copy(g[:, b % 2, :, :], acc_h[:, ds(t * 4, 4), 0:C]).then_inc(s_g, 1)

            def residual(t, b):
                pool.wait_ge(s_in[b], filled(t, b, RG, 64))
                if past(t, RG):
                    pool.wait_ge(s_out, t - RG + 1)
                pool.tensor_tensor(xb[:, b, :], x[:, b, :], blang[:, :], ALU.add).then_inc(s_xb, 1)

            pool.wait_ge(s_w, 80)
            pipeline(pool, TILES, RG, [(0, take), (1, residual)])

        @block.sync
        def _(sp):
            sp.dma_start(w_c[:, 0:C], T.W_cross).then_inc(s_w, 16)
            sp.dma_start(w_cT[:, :], T.W_crossT).then_inc(s_w, 16)
            sp.dma_start(att[:, :], T.att).then_inc(s_w, 16)
            sp.dma_start(blang[:, :], T.bias_lang.rearrange("(a c) -> a c", a=1).to_broadcast([P, C])).then_inc(s_w, 16)
            sp.dma_start(valid[:, :, :], T.valid.rearrange("(t p) r -> p t r", p=P)).then_inc(s_w, 16)

            def load(t, b):
                if past(t, RG):
                    sp.wait_ge(s_out, t - RG + 1)
                sp.dma_start(x[:, b, :], T.x[ds(t * P, P), :]).then_inc(s_in[b], 16)
                sp.dma_start(ent[:, b, 0, :], T.srow[ds(t * P, P), 0:C]).then_inc(s_in[b], 16)
                sp.dma_start(ls[:, b, 0, :], T.srow[ds(t * P, P), C:CR]).then_inc(s_in[b], 16)
                sp.dma_start(ld[:, b, :], T.srow[ds(t * P, P), CR:CR + H]).then_inc(s_in[b], 16)

            def store(t, b):
                sp.wait_ge(s_out, t + 1)
                sp.dma_start(T.x1[ds(t * P, P), :], out[:, b % 2, :]).then_inc(s_st[b % 2], 16)

            pipeline(sp, TILES, RG, [(0, load), (3, store)])
            for b in range(2):
                sp.wait_ge(s_st[b], 16 * (TILES // 2))

        @block.vector
        def _(dve):
            dve.wait_ge(s_w, 80)
            dve.tensor_scalar(adiag[:, :], K.headmask[:, :], att[:, 2 * R:2 * R + 1], None, ALU.mult).then_inc(s_adiag, 1)
            dve.tensor_scalar(hide[:, :, :], valid[:, :, :], 1.0, BIG, ALU.subtract, ALU.mult).then_inc(s_adiag, 1)
            dve.wait_ge(s_fold, 1)
            dve.tensor_copy(w_c[:, C:CR], f_ps[:, :]).then_inc(s_wc, 1)
            dve.wait_ge(s_adiag, 2)
            c, e, f = Chain(dve, s_c, 4), Chain(dve, s_gend, 5), Chain(dve, s_stat, 4)

            def logits(t, b, step):
                if step == 0:
                    dve.wait_ge(s_ent, t + 1)
                    if past(t, 1):
                        dve.wait_ge(s_arg, t)
                    dve.wait_ge(s_in[b], filled(t, b, RG, 64))
                    c.group(t)
                    ins = dve.tensor_tensor(t1[:, :, :], ls[:, b, :, :],
                                            ld[:, b, :].unsqueeze(1).to_broadcast([P, M, H]), ALU.add)
                else:
                    dve.wait_ge(s_c, t * 4 + step)
                    if step == 1:
                        ins = dve.scalar_tensor_tensor(t1[:, :, :], t1[:, :, :], SLOPE0, t1[:, :, :], ALU.mult, ALU.max)
                    elif step == 2:
                        hidden = hide[:, ds(t, 1), :].rearrange("p a r -> p (a r)").unsqueeze(2)
                        ins = dve.tensor_tensor(t1[:, 1:M, :], t1[:, 1:M, :], hidden.to_broadcast([P, R, H]), ALU.add)
                    elif step == 3:
                        ins = dve.tensor_reduce(top[:, :], t1[:, :, :].rearrange("p m h -> p h m"), AX.X, ALU.max)
                    else:
                        dve.tensor_tensor(al[:, b % 2, :, :], t1[:, :, :], top[:, :].unsqueeze(1).to_broadcast([P, M, H]),
                                          ALU.subtract).then_inc(s_arg, 1)
                        return
                c.mark(ins)

            def mix(t, b, step):
                if step == 0:
                    dve.wait_ge(s_ex, t + 1)
                    e.group(t)
                    ins = dve.tensor_reduce(den[:, :], ex[:, b % 2, :, :].rearrange("p m h -> p h m"), AX.X, ALU.add)
                else:
                    dve.wait_ge(s_gend, t * 5 + step)
                    if step == 1:
                        ins = dve.reciprocal(den[:, :], den[:, :])
                    elif step == 2:
                        ins = dve.tensor_tensor(ex[:, b % 2, :, :], ex[:, b % 2, :, :],
                                                den[:, :].unsqueeze(1).to_broadcast([P, M, H]), ALU.mult)
                    elif step == 3:
                        ins = dve.tensor_tensor(prod[:, :, :].rearrange("p m (h d) -> p (m h) d", h=H),
                                                ent[:, b, :, :].rearrange("p m (h d) -> p (m h) d", h=H),
                                                flat(ex[:, b % 2, :, :]).unsqueeze(2).to_broadcast([P, M * H, D]), ALU.mult)
                    elif step == 4:
                        ins = dve.tensor_reduce(mixed[:, :], prod[:, :, :].rearrange("p m c -> p c m"), AX.X, ALU.add)
                    else:
                        dve.wait_ge(s_xb, t + 1)
                        if past(t, 2):
                            dve.wait_ge(s_st[b % 2], (t - b % 2) * 8)
                        dve.tensor_tensor(out[:, b % 2, :], mixed[:, :], xb[:, b, :], ALU.add).then_inc(s_out, 1)
                        return
                e.mark(ins)

            def statistics(t, b, step):
                if step == 0:
                    dve.wait_ge(s_out, t + 1)
                    f.group(t)
                    f.mark(dve.bn_stats(stats[:, :], out[:, b % 2, :]))
                elif step == 1:
                    dve.wait_ge(s_stat, t * 4 + 1)
                    settle(dve, K)
                    f.mark(dve.bn_aggr(mv[:, :], stats[:, :]))
                else:
                    dve.wait_ge(s_stat, t * 4 + 2)
                    f.mark(dve.tensor_copy(K.mean[:, ds(t, 1)], mv[:, 0:1]))
                    f.mark(dve.tensor_scalar(K.var[:, ds(t, 1)], mv[:, 1:2], EPS, None, ALU.add))

            def tick(t, h, has):
                for step in range(6):
                    if has(0) and step < 5:
                        logits(t, h, step)
                    if has(1):
                        mix(t - 1, (h - 1) % RG, step)
                    if has(2) and step < 3:
                        statistics(t - 2, (h - 2) % RG, step)

            ticks(dve, TILES, RG, 2, tick)
            dve.wait_ge(s_stat, 4 * TILES)

        @block.scalar
        def _(act):
            def move(t, b):
                act.wait_ge(s_gT, t + 1)
                if past(t, 2):
                    act.wait_ge(s_h, t - 1)
                act.activation(gT[:, b % 2, :], gT_ps[b % 2][:, :], ACT.Copy).then_inc(s_gTs, 1)

            def entries(t, b):
                act.wait_ge(s_h, t + 1)
                if past(t, RG):
                    act.wait_ge(s_out, t - RG + 1)
                for q in range(2):
                    act.activation(ent[:, b, 1 + 2 * q:3 + 2 * q, :], h_ps[b % 2][q][:, :, 0:C], ACT.Copy)
                    last = act.activation(ls[:, b, 1 + 2 * q:3 + 2 * q, :], h_ps[b % 2][q][:, :, C:CR], ACT.Copy)
                last.then_inc(s_ent, 1)

            def exponentials(t, b):
                act.wait_ge(s_arg, t + 1)
                if past(t, 2):
                    act.wait_ge(s_out, t - 1)
                act.activation(ex[:, b % 2, :, :], al[:, b % 2, :, :], ACT.Exp).then_inc(s_ex, 1)

            pipeline(act, TILES, RG, [(0, move), (1, entries), (2, exponentials)])

        @block.tensor
        def _(pe):
            pe.wait_ge(s_w, 80)
            pe.wait_ge(s_adiag, 1)
            pe.matmul(f_ps[:, :], w_cT[:, :], adiag[:, :], start=True, stop=True).then_inc(s_fold, 1)
            pe.wait_ge(s_wc, 1)

            def transpose(t, b):
                if past(t, 2):
                    pe.wait_ge(s_gTs, t - 1)
                pe.wait_ge(s_g, t + 1)
                for u in range(4):
                    last = pe.transpose(gT_ps[b % 2][:, u * P:(u + 1) * P], g[:, b % 2, u, :], K.ident[:, :])
                last.then_inc(s_gT, 1)

            def project(t, b):
                pe.wait_ge(s_gTs, t + 1)
                if past(t, 2):
                    pe.wait_ge(s_ent, t - 1)
                g4 = gT[:, b % 2, :].rearrange("f (n r) -> f r n", r=R)
                for r in range(R):
                    last = pe.matmul(h_ps[b % 2][r // 2][:, r % 2, :], g4[:, r, :], w_c[:, :], start=True, stop=True)
                last.then_inc(s_h, 1)

            pipeline(pe, TILES, RG, [(0, transpose), (1, project)])


def edge_inputs(nc, K, T, h1T):
    with Phase(nc, "edgein") as ph:
        XCH = 10
        x = ph.sb("x", [P, TILES, C])
        rstd = ph.sb("rstd", [P, TILES])
        nmr = ph.sb("nmr", [P, TILES])
        w = ph.sb("w", [P, 2, HID])
        h = ph.sb("h", [P, 2, C])
        hT = ph.sb("hT", [P, 2, P])
        ab = ph.sb("ab", [P, 2, 2 * HID])
        hT_ps = [ph.ps(f"hT_ps{b}", [P, P]) for b in range(2)]
        ab_ps = [ph.ps(f"ab_ps{b}", [P, 2 * HID]) for b in range(2)]
        s_w, s_x, s_sd, s_norm, s_h, s_hT, s_hTs, s_ab, s_abs = (
            ph.sem(n) for n in ("w", "x", "sd", "norm", "h", "hT", "hTs", "ab", "abs"))
        s_st = [ph.sem(f"st{b}") for b in range(2)]
        valid = ph.sb("valid", [P, STEPS])
        inside = ph.sb("inside", [P, STEPS])
        srci = ph.sb("srci", [P, STEPS], I32)
        part = ph.sb("part", [P, STEPS], I32)
        block = ph.block()

        @block.sync
        def _(sp):
            for c in range(0, TILES, XCH):
                sp.dma_start(x[:, c:c + XCH, :], T.x1.rearrange("(t p) c -> p t c", p=P)[:, c:c + XCH, :]).then_inc(s_x, 16)
            sp.dma_start(w[:, :, :], T.We1[0:2 * C, :].rearrange("(s i) o -> i s o", s=2)).then_inc(s_w, 16)

            def store(t, b):
                sp.wait_ge(s_abs, t + 1)
                sp.dma_start(T.ab[ds(t * P, P), :], ab[:, b, :]).then_inc(s_st[b], 16)

            pipeline(sp, TILES, 2, [(0, store)])
            for b in range(2):
                sp.wait_ge(s_st[b], 16 * (TILES // 2))

        @block.vector
        def _(dve):
            L = K.setup.on(dve)
            dve.wait_ge(s_sd, 1)
            L.link(dve.reciprocal(rstd[:, :], rstd[:, :]))
            dve.scalar_tensor_tensor(nmr[:, :], K.mean[:, :], -1.0, rstd[:, :], ALU.mult, ALU.mult).then_inc(s_norm, 1)

            L.mark(dve.tensor_scalar(valid[:, :], K.loc[:, :], 0.0, None, ALU.is_ge))
            L.link(dve.tensor_scalar(inside[:, :], K.loc[:, :], float(WIN), None, ALU.is_lt))
            L.link(dve.tensor_tensor(valid[:, :], valid[:, :], inside[:, :], ALU.mult))
            L.link(dve.scalar_tensor_tensor(K.srcv[:, :], K.src[:, :], 1.0, valid[:, :], ALU.add, ALU.mult))
            L.mark(dve.scalar_tensor_tensor(K.rowd[:, :], K.src[:, :], K.trash[:, 0:1], valid[:, :], ALU.subtract, ALU.mult))
            L.link(dve.tensor_copy(srci[:, :], K.srcv[:, :]))
            L.link(dve.tensor_scalar(part[:, :], srci[:, :], 7, None, ALU.arith_shift_right))
            L.link(dve.tensor_copy(K.src_hl[:, :, 0], part[:, :]))
            L.link(dve.tensor_scalar(part[:, :], srci[:, :], P - 1, None, ALU.bitwise_and))
            L.link(dve.tensor_copy(K.src_hl[:, :, 1], part[:, :]))

            def evacuate(t, b):
                dve.wait_ge(s_hT, t + 1)
                if past(t, 2):
                    dve.wait_ge(s_ab, t - 1)
                dve.tensor_copy(h1T[:, ds(t * P, P)], hT_ps[b][:, :])
                dve.tensor_copy(hT[:, b, :], hT_ps[b][:, :]).then_inc(s_hTs, 1)

            pipeline(dve, TILES, 2, [(0, evacuate)])

        @block.scalar
        def _(act):
            act.activation(rstd[:, :], K.var[:, :], ACT.Sqrt).then_inc(s_sd, 1)
            act.wait_ge(s_norm, 1)
            act.wait_ge(s_x, 16 * (TILES // XCH))

            def normalize(t, b):
                if past(t, 2):
                    act.wait_ge(s_hT, t - 1)
                act.activation(h[:, b, :], x[:, ds(t, 1), :].rearrange("p a c -> p (a c)"), ACT.Relu,
                               bias=nmr[:, ds(t, 1)], scale=rstd[:, ds(t, 1)]).then_inc(s_h, 1)

            def evacuate(t, b):
                act.wait_ge(s_ab, t + 1)
                if past(t, 2):
                    act.wait_ge(s_st[b], (t - b) * 8)
                act.activation(ab[:, b, :], ab_ps[b][:, :], ACT.Copy).then_inc(s_abs, 1)

            pipeline(act, TILES, 2, [(0, normalize), (2, evacuate)])

        @block.tensor
        def _(pe):
            pe.wait_ge(s_w, 16)

            def transpose(t, b):
                pe.wait_ge(s_h, t + 1)
                if past(t, 2):
                    pe.wait_ge(s_hTs, t - 1)
                pe.transpose(hT_ps[b][:, :], h[:, b, :], K.ident[:, :]).then_inc(s_hT, 1)

            def products(t, b):
                pe.wait_ge(s_hTs, t + 1)
                if past(t, 2):
                    pe.wait_ge(s_abs, t - 1)
                pe.matmul(ab_ps[b][:, :], hT[:, b, :], flat(w[:, :, :]), start=True, stop=True).then_inc(s_ab, 1)

            pipeline(pe, TILES, 2, [(0, transpose), (1, products)])


def edge_messages(nc, K, T, fwd):
    with Phase(nc, "msg") as ph:
        U, RG = 4, 4
        GROUPS = STEPS // U
        SUM_LAG, ADD_LAG = 2, 3
        idx = ph.sb("idx", [P, RG, U], I32)
        sidx = ph.sb("sidx", [P, RG, U], I32)
        hl = ph.sb("hl", [P, RG, U, 2], BF16)
        dup = ph.sb("dup", [P, RG, U])
        rowf = ph.sb("rowf", [P, U])
        onehot = ph.sb("onehot", [P, RG, U, WIN])
        same = ph.sb("same", [P, 2, U, P])
        ga = ph.sb("ga", [P, RG, U, 2 * HID])
        lt = ph.sb("lt", [P, RG, U, P])
        rw = ph.sb("rw", [P, 2, U, 2 * HID])
        xs = ph.sb("xs", [P, 2, 2 * HID])
        hid = ph.sb("hid", [P, 2, U, 2 * HID])
        bsum = ph.sb("bsum", [P, RG, U, HID])
        oT_ps = ph.ps("oT_ps", [WIN, U * P])
        src_ps = ph.ps("src_ps", [P, U, P])
        pre_ps = [ph.ps(f"pre_ps{b}", [P, 2 * HID]) for b in range(2)]
        fwd_ps = [ph.ps(f"fwd_ps{b}", [P, 2 * WIN]) for b in range(2)]
        bwd_ps = [ph.ps(f"bwd_ps{b}", [P, HID]) for b in range(2)]
        s_ga = [ph.sem(f"ga{b}") for b in range(RG)]
        s_ef = [ph.sem(f"ef{b}") for b in range(RG)]
        s_rw = [ph.sem(f"rw{b}") for b in range(2)]
        s_sum = [ph.sem(f"sum{u}") for u in range(U)]
        (s_w, s_idx, s_oh, s_tr, s_oT, s_same, s_row, s_pre, s_x, s_hid, s_edge, s_acc, s_bs, s_rc) = (
            ph.sem(n) for n in ("w", "idx", "oh", "tr", "oT", "same", "row", "pre", "x", "hid", "edge", "acc", "bs", "rc"))
        block = ph.block()

        @block.sync
        def _(sp):
            for b in range(2):
                for u in range(U):
                    for q in range(2):
                        sp.dma_start(rw[WIN:P, b, u, q * HID:(q + 1) * HID], T.We1[2 * C:2 * C + EF, :]).then_inc(s_w, 16)
            sp.wait_ge(s_w, 16 * 4 * U)

            def features(j, b):
                e = registers(nc, sp, mybir.EngineType.SP, K.reg_e, j * U, U, N_EDGES)
                if past(j, RG):
                    sp.wait_ge(s_pre, (j - RG + 1) * U)
                    settle(sp, K)
                for u in range(U):
                    sp.dma_start(lt[WIN:P, b, u, :], T.efT[:, ds(e[u], P)]).then_inc(s_ef[b], 16)

            def windows(j, b):
                w = registers(nc, sp, mybir.EngineType.SP, K.reg_w, j * U, U, WINDOWS - 1)
                if past(j, 2):
                    sp.wait_ge(s_pre, (j - 1) * U)
                    settle(sp, K)
                for u in range(U):
                    sp.dma_start(rw[0:WIN, b % 2, u, :], T.ab[ds(w[u] * WIN, WIN), :]).then_inc(s_rw[b % 2], 16)

            pipeline(sp, GROUPS, RG, [(0, features), (0, windows)])

        @block.gpsimd
        def _(pool):
            def scatter(j, b, u):
                if u == 0:
                    pool.wait_ge(s_row, j + 1)
                pool.wait_ge(s_bs, j * U + u + 1)
                if u >= 2:
                    pool.wait_ge(s_sum[u - 2], (j + 1) * 16)
                elif past(j, 1):
                    pool.wait_ge(s_sum[u + 2], j * 16)
                settle(pool, K)
                pool.indirect_dma_start(T.sums[u % 2], bass.IndirectOffsetOnAxis(ap=sidx[:, b, u:u + 1], axis=0),
                                        bsum[:, b, u, :], None, compute_op=ALU.add).then_inc(s_sum[u], 16)

            def gather(j, b, u):
                if u == 0:
                    pool.wait_ge(s_idx, j + 1)
                if past(j, RG):
                    pool.wait_ge(s_x, (j - RG) * U + u + 1)
                settle(pool, K)
                pool.indirect_dma_start(ga[:, b, u, :], None, T.ab,
                                        bass.IndirectOffsetOnAxis(ap=idx[:, b, u:u + 1], axis=0)).then_inc(s_ga[b], 16)

            stages = []
            for u in range(U):
                stages += [(4, lambda j, b, u=u: scatter(j, b, u)), (0, lambda j, b, u=u: gather(j, b, u))]
            pipeline(pool, GROUPS, RG, stages)
            for u in range(U):
                pool.wait_ge(s_sum[u], 16 * GROUPS)

        @block.vector
        def _(dve):
            rc = Chain(dve, s_rc, 1)

            windows = Windows(nc, dve, mybir.EngineType.DVE, K, U, RG, 2)

            def hots(j, b):
                if past(j, RG):
                    dve.wait_ge(s_edge, (j - RG + 1) * U)
                k = ds(j * U, U)
                dve.tensor_copy(hl[:, b, :, :], K.src_hl[:, k, :])
                dve.tensor_tensor(onehot[:, b, :, :], K.ramp[:, 0:WIN].unsqueeze(1).to_broadcast([P, U, WIN]),
                                  K.loc[:, k].unsqueeze(2).to_broadcast([P, U, WIN]), ALU.is_equal).then_inc(s_oh, 1)

            def compare(j, b, u):
                if u == 0:
                    dve.wait_ge(s_tr, j + 1)
                if past(j, 2):
                    dve.wait_ge(s_edge, (j - 2) * U + u + 1)
                dve.scalar_tensor_tensor(same[:, b % 2, u, :], src_ps[:, u, :], K.srcv[:, ds(j * U + u, 1)], K.upto[:, :],
                                         ALU.is_equal, ALU.mult, accum_out=dup[:, b, u:u + 1]).then_inc(s_same, 1)

            def rows(j, b):
                if isinstance(j, int) and j == 0:
                    for u in range(U):
                        compare(j, b, u)
                dve.wait_ge(s_same, (j + 1) * U)
                rc.group(j)
                rc.link(dve.scalar_tensor_tensor(rowf[:, :], dup[:, b, :], 1.0, K.rowd[:, ds(j * U, U)], ALU.is_equal, ALU.mult))
                if past(j, RG):
                    for u in range(U):
                        dve.wait_ge(s_sum[u], (j - RG + 1) * 16)
                dve.tensor_scalar(sidx[:, b, :], rowf[:, :], K.trash[:, 0:1], None, ALU.add).then_inc(s_row, 1)

            def add(n, u, w):
                dve.wait_ge(s_edge, n + 1)
                dve.wait_ge(s_acc, n + 1)
                dst = fwd[:, ds(w, 1), :, :].rearrange("f a c n -> f (a c n)")
                dve.tensor_tensor(dst, dst, fwd_ps[u % 2][:, :], ALU.add).then_inc(s_acc, 1)

            def steps(j, b):
                first, final = isinstance(j, int) and j == 0, isinstance(j, int) and j == GROUPS - 1
                w = windows.of(j, b, ADD_LAG)
                if first:
                    dve.memset(fwd[:, :, :, :], 0.0).then_inc(s_acc, 1)
                for u in range(U):
                    n = j * U + u
                    if not first or u >= ADD_LAG:
                        add(n - ADD_LAG, (u - ADD_LAG) % U, w[u])
                    if u == 0:
                        dve.wait_ge(s_ga[b], filled(j, b, RG, 16 * U))
                    dve.wait_ge(s_pre, n + 1)
                    if past(j, 1) or u >= 2:
                        dve.wait_ge(s_hid, n - 1)
                    dve.tensor_tensor(xs[:, u % 2, 0:HID], pre_ps[u % 2][:, 0:HID], ga[:, b, u, HID:2 * HID], ALU.add)
                    dve.tensor_tensor(xs[:, u % 2, HID:2 * HID], pre_ps[u % 2][:, HID:2 * HID], ga[:, b, u, 0:HID],
                                      ALU.add).then_inc(s_x, 1)
                    if not final:
                        compare(j + 1, (b + 1) % RG, u)
                    dve.wait_ge(s_x, n + 1)
                    if past(j, 2):
                        dve.wait_ge(s_edge, (j - 2) * U + u + 1)
                    dve.scalar_tensor_tensor(hid[:, b % 2, u, :], xs[:, u % 2, :], SLOPE1, xs[:, u % 2, :],
                                             ALU.mult, ALU.max).then_inc(s_hid, 1)

            pipeline(dve, GROUPS, RG, [(0, hots), (2, steps), (1, rows)])
            w = registers(nc, dve, mybir.EngineType.DVE, K.reg_w, STEPS - ADD_LAG, ADD_LAG, WINDOWS - 1)
            for n in range(STEPS - ADD_LAG, STEPS):
                add(n, n % U, w[n - STEPS + ADD_LAG])
            dve.wait_ge(s_acc, STEPS + 1)

        @block.scalar
        def _(act):
            def indices(j, b):
                if past(j, RG):
                    act.wait_ge(s_ga[b], filled(j, b, RG, 16 * U) - 16 * U)
                act.activation(idx[:, b, :], K.src[:, ds(j * U, U)], ACT.Copy).then_inc(s_idx, 1)

            def move(j, b):
                act.wait_ge(s_tr, j + 1)
                if past(j, RG):
                    act.wait_ge(s_pre, (j - RG + 1) * U)
                act.activation(lt[0:WIN, b, :, :], oT_ps[:, :].rearrange("n (u p) -> n u p", u=U), ACT.Copy).then_inc(s_oT, 1)

            def sums(j, b):
                for u in range(U):
                    act.wait_ge(s_edge, j * U + u + 1)
                    if past(j, RG):
                        act.wait_ge(s_sum[u], (j - RG + 1) * 16)
                    act.activation(bsum[:, b, u, :], bwd_ps[u % 2][:, :], ACT.Copy).then_inc(s_bs, 1)

            pipeline(act, GROUPS, RG, [(0, indices), (4, sums), (2, move)])

        @block.tensor
        def _(pe):
            pe.wait_ge(s_w, 16 * 4 * U)

            def transpose(j, b):
                pe.wait_ge(s_oh, j + 1)
                if past(j, 1):
                    pe.wait_ge(s_oT, j)
                    pe.wait_ge(s_same, j * U)
                settle(pe, K)
                for u in range(U):
                    pe.transpose(oT_ps[:, u * P:(u + 1) * P], onehot[:, b, u, :], K.ident[:, :])
                for u in range(U):
                    pe.matmul(src_ps[:, u, :], hl[:, b, u, 0:1].to_broadcast([P, P]), K.identb128[:, :], start=True, stop=False)
                    last = pe.matmul(src_ps[:, u, :], hl[:, b, u, 1:2].to_broadcast([P, P]), K.identb[:, :], start=False, stop=True)
                last.then_inc(s_tr, 1)

            def after(n, j, b, u):
                pe.wait_ge(s_hid, n + 1)
                pe.wait_ge(s_same, n + 1)
                if past(j, 1) or u >= 2:
                    pe.wait_ge(s_acc, n)
                    pe.wait_ge(s_bs, n - 1)
                for q in range(2):
                    pe.matmul(fwd_ps[u % 2][:, q * WIN:(q + 1) * WIN], hid[:, b % 2, u, HID + q * P:HID + (q + 1) * P],
                              onehot[:, b, u, :], start=True, stop=True)
                pe.matmul(bwd_ps[u % 2][:, :], same[:, b % 2, u, :], hid[:, b % 2, u, 0:HID],
                          start=True, stop=True).then_inc(s_edge, 1)

            def steps(j, b):
                pe.wait_ge(s_oT, j + 1)
                pe.wait_ge(s_ef[b], filled(j, b, RG, 16 * U))
                pe.wait_ge(s_rw[b % 2], (j // 2 + 1) * 16 * U if isinstance(j, int) else (j - b % 2) * 8 * U + 16 * U)
                for u in range(U):
                    n = j * U + u
                    if past(j, 1) or u >= 2:
                        pe.wait_ge(s_x, n - 1)
                    pe.matmul(pre_ps[u % 2][:, :], lt[:, b, u, :], rw[:, b % 2, u, :], start=True, stop=True).then_inc(s_pre, 1)
                    if u >= SUM_LAG:
                        after(n - SUM_LAG, j, b, u - SUM_LAG)
                    elif past(j, 1):
                        after(n - SUM_LAG, j - 1, (b - 1) % RG, u - SUM_LAG + U)
                    if u == 0 and not (isinstance(j, int) and j == GROUPS - 1):
                        transpose(j + 1, (b + 1) % RG)

            transpose(0, 0)
            pipeline(pe, GROUPS, RG, [(1, steps)])
            for n in range(STEPS - SUM_LAG, STEPS):
                after(n, GROUPS - 1, (GROUPS - 1) % RG, n % U)


def outputs(nc, K, T, fwd, h1T):
    with Phase(nc, "out") as ph:
        tab = ph.sb("tab", [P, 2, 2, HID])
        bsum = ph.sb("bsum", [P, 2, HID])
        x = ph.sb("x", [P, 2, C])
        hsum = ph.sb("hsum", [P, 2, 2, P])
        red = ph.sb("red", [P, 2, P])
        z = ph.sb("z", [P, 2, 2, P])
        zl = ph.sb("zl", [P, 2, 2, P])
        y = ph.sb("y", [P, 2, C])
        we2 = ph.sb("we2", [P, 2, C])
        wn1 = ph.sb("wn1", [P, 2, HID])
        wn2 = ph.sb("wn2", [P, 2, C])
        bT_ps = [ph.ps(f"bT_ps{b}", [P, 2, P]) for b in range(2)]
        red_ps = [ph.ps(f"red_ps{b}", [P, P]) for b in range(2)]
        z_ps = [ph.ps(f"z_ps{b}", [P, 2, P]) for b in range(2)]
        y_ps = [ph.ps(f"y_ps{b}", [P, C]) for b in range(2)]
        s_in = [ph.sem(f"in{b}") for b in range(2)]
        s_xin = [ph.sem(f"xin{b}") for b in range(2)]
        s_st = [ph.sem(f"st{b}") for b in range(2)]
        s_w, s_b, s_bT, s_hs, s_red, s_reds, s_z, s_zs, s_zl, s_y, s_out = (
            ph.sem(n) for n in ("w", "b", "bT", "hs", "red", "reds", "z", "zs", "zl", "y", "o"))
        block = ph.block()

        @block.sync
        def _(sp):
            sp.dma_start(we2[:, :, :], T.We2.rearrange("(q i) o -> i q o", q=2)).then_inc(s_w, 16)
            sp.dma_start(wn1[:, :, :], T.Wn1.rearrange("(q i) o -> i q o", q=2)).then_inc(s_w, 16)
            sp.dma_start(wn2[:, :, :], T.Wn2.rearrange("(q i) o -> i q o", q=2)).then_inc(s_w, 16)

            def load(t, b):
                if past(t, 2):
                    sp.wait_ge(s_b, t - 1)
                for q in range(2):
                    sp.dma_start(tab[:, b, q, :], T.sums[q][ds(t * P, P), :]).then_inc(s_in[b], 16)

            def load_x(t, b):
                if past(t, 2):
                    sp.wait_ge(s_out, t - 1)
                sp.dma_start(x[:, b, :], T.x1[ds(t * P, P), :]).then_inc(s_xin[b], 16)

            def store(t, b):
                sp.wait_ge(s_out, t + 1)
                sp.dma_start(T.out[ds(t * P, P), :], y[:, b, :]).then_inc(s_st[b], 16)

            pipeline(sp, TILES, 2, [(0, load), (3, load_x), (5, store)])
            for b in range(2):
                sp.wait_ge(s_st[b], 16 * (TILES // 2))

        @block.vector
        def _(dve):
            def gather(t, b):
                dve.wait_ge(s_in[b], filled(t, b, 2, 32))
                if past(t, 2):
                    dve.wait_ge(s_bT, t - 1)
                dve.tensor_tensor(bsum[:, b, :], tab[:, b, 0, :], tab[:, b, 1, :], ALU.add).then_inc(s_b, 1)

            def both(t, b):
                dve.wait_ge(s_bT, t + 1)
                if past(t, 2):
                    dve.wait_ge(s_red, t - 1)
                for q in range(2):
                    last = dve.tensor_tensor(hsum[:, b, q, :].rearrange("f (w n) -> f w n", n=WIN),
                                             bT_ps[b][:, q, :].rearrange("f (w n) -> f w n", n=WIN),
                                             fwd[:, ds(t * 2, 2), q, :], ALU.add)
                last.then_inc(s_hs, 1)

            def activate(t, b):
                dve.wait_ge(s_zs, t + 1)
                if past(t, 2):
                    dve.wait_ge(s_y, t - 1)
                dve.scalar_tensor_tensor(zl[:, b, :, :], z[:, b, :, :], SLOPE1, z[:, b, :, :], ALU.mult, ALU.max).then_inc(s_zl, 1)

            def residual(t, b):
                dve.wait_ge(s_y, t + 1)
                dve.wait_ge(s_xin[b], filled(t, b, 2, 16))
                if past(t, 2):
                    dve.wait_ge(s_st[b], (t - b) * 8)
                dve.tensor_tensor(y[:, b, :], y_ps[b][:, :], x[:, b, :], ALU.add).then_inc(s_out, 1)

            dve.wait_ge(s_w, 48)
            pipeline(dve, TILES, 2, [(4, residual), (3, activate), (1, both), (0, gather)])

        @block.scalar
        def _(act):
            def reduced(t, b):
                act.wait_ge(s_red, t + 1)
                if past(t, 2):
                    act.wait_ge(s_z, t - 1)
                act.activation(red[:, b, :], red_ps[b][:, :], ACT.Copy).then_inc(s_reds, 1)

            def hidden(t, b):
                act.wait_ge(s_z, t + 1)
                if past(t, 2):
                    act.wait_ge(s_zl, t - 1)
                act.activation(z[:, b, :, :], z_ps[b][:, :, :], ACT.Copy).then_inc(s_zs, 1)

            pipeline(act, TILES, 2, [(1, hidden), (0, reduced)])

        @block.tensor
        def _(pe):
            pe.wait_ge(s_w, 48)

            def transpose(t, b):
                pe.wait_ge(s_b, t + 1)
                if past(t, 2):
                    pe.wait_ge(s_hs, t - 1)
                for q in range(2):
                    last = pe.transpose(bT_ps[b][:, q, :], bsum[:, b, q * P:(q + 1) * P], K.ident[:, :])
                last.then_inc(s_bT, 1)

            def reduce(t, b):
                pe.wait_ge(s_hs, t + 1)
                if past(t, 2):
                    pe.wait_ge(s_reds, t - 1)
                for q in range(2):
                    last = pe.matmul(red_ps[b][:, :], we2[:, q, :], hsum[:, b, q, :], start=(q == 0), stop=(q == 1))
                last.then_inc(s_red, 1)

            def hidden(t, b):
                pe.wait_ge(s_reds, t + 1)
                if past(t, 2):
                    pe.wait_ge(s_zs, t - 1)
                for q in range(2):
                    pe.matmul(z_ps[b][:, q, :], wn1[:, 0, q * P:(q + 1) * P], h1T[:, ds(t * P, P)], start=True, stop=False)
                    last = pe.matmul(z_ps[b][:, q, :], wn1[:, 1, q * P:(q + 1) * P], red[:, b, :], start=False, stop=True)
                last.then_inc(s_z, 1)

            def output(t, b):
                pe.wait_ge(s_zl, t + 1)
                if past(t, 2):
                    pe.wait_ge(s_out, t - 1)
                for q in range(2):
                    last = pe.matmul(y_ps[b][:, :], zl[:, b, q, :], wn2[:, q, :], start=(q == 0), stop=(q == 1))
                last.then_inc(s_y, 1)

            pipeline(pe, TILES, 2, [(3, output), (2, hidden), (1, reduce), (0, transpose)])


class Namespace:
    pass


def build(nc, T):
    with Phase(nc, "k") as ph:
        K = Namespace()
        K.ramp, K.part, K.grid = ph.sb("ramp", [P, 256]), ph.sb("part", [P, 1]), ph.sb("grid", [P, KC])
        K.ident, K.upto, K.ones = ph.sb("ident", [P, P]), ph.sb("upto", [P, P]), ph.sb("ones", [P, P])
        K.identb, K.identb128 = ph.sb("identb", [P, P], BF16), ph.sb("identb128", [P, P], BF16)
        K.headmask, K.trash = ph.sb("headmask", [P, H]), ph.sb("trash", [P, 1])
        K.reg_w, K.reg_e = ph.sb("reg_w", [1, P * KC], I32), ph.sb("reg_e", [1, P * KC], I32)
        K.loc, K.src = ph.sb("loc", [P, STEPS]), ph.sb("src", [P, STEPS], I32)
        K.mean, K.var = ph.sb("mean", [P, TILES]), ph.sb("var", [P, TILES])
        K.passed = ph.sem("passed")
        K.setup = Links(None, ph.sem("setup"))
        constants(nc, K)
        with Phase(nc, "l0") as l0:
            K.key, K.typ, K.idx = l0.sb("key", [P, STEPS]), l0.sb("typ", [P, STEPS]), l0.sb("idx", [P, STEPS], I32)
            with Phase(nc, "ed") as e:
                K.wbase, K.wstep_i = e.sb("wbase", [P, STEPS]), e.sb("wstep_i", [P, STEPS], I32)
                K.ed = e.sb("ed", [WIN, WSLOTS, R * H])
                schedule(nc, K, T)
                node_inputs(nc, K, T)
                relation_maxima(nc, K, T)
            acc = l0.sb("acc", [P, WSLOTS, 2, XR])
            relation_attention(nc, K, T, acc)
            node_update(nc, K, T, acc)
        with Phase(nc, "l1") as l1:
            K.srcv, K.rowd = l1.sb("srcv", [P, STEPS]), l1.sb("rowd", [P, STEPS])
            K.src_hl = l1.sb("src_hl", [P, STEPS, 2], BF16)
            h1T = l1.sb("h1T", [P, NP])
            edge_inputs(nc, K, T, h1T)
            fwd = l1.sb("fwd", [P, WSLOTS, 2, WIN])
            edge_messages(nc, K, T, fwd)
            outputs(nc, K, T, fwd, h1T)


def kernel(x, src, dst, edge_attr_64, edge_type_4, L0_gnn_W_rel, L0_gnn_att_src_rel, L0_gnn_att_dst_rel, L0_gnn_bias_rel,
           L0_gnn_W_self, L0_gnn_W_cross, L0_gnn_att_src_lang, L0_gnn_att_dst_lang, L0_gnn_bias_lang,
           L1_gnn_We1, L1_gnn_We2, L1_gnn_Wn1, L1_gnn_Wn2):
    import numpy as np
    import concourse.bacc as bacc
    from concourse.bass_utils import run_bass_kernel_spmd as run

    nc = bacc.Bacc("TRN2", target_bir_lowering=False, num_devices=1)
    asn = np.ascontiguousarray
    src, dst, typ = (np.asarray(a).astype(np.int32) for a in (src, dst, edge_type_4))

    rec = np.zeros((EPAD, REC), np.int32)
    rec[:, 1] = rec[:, 3] = rec[:, 4] = PAD_DST
    rec[:N_EDGES, 0], rec[:N_EDGES, 1], rec[:N_EDGES, 2] = src, dst, typ
    rec[1:, 3], rec[:-1, 4] = rec[:-1, 1], rec[1:, 1]
    all_dst = np.full((BLOCKS, P), PAD_DST, np.int32)
    all_dst.reshape(-1)[:N_EDGES] = dst
    xp = np.zeros((NP, C), np.float32)
    xp[:N_NODES] = x
    efT = np.zeros((EF, EPAD), np.float32)
    efT[:, :N_EDGES] = np.asarray(edge_attr_64).T
    a_s, a_d = (np.asarray(a).reshape(R, C) for a in (L0_gnn_att_src_rel, L0_gnn_att_dst_rel))
    l_s, l_d = (np.asarray(a).reshape(1, C) for a in (L0_gnn_att_src_lang, L0_gnn_att_dst_lang))
    att = asn(np.concatenate([np.stack([a_s, a_d], axis=1).reshape(2 * R, C), l_s, l_d]).T)

    given = {
        "x": xp, "rec": rec, "dst": all_dst, "first": asn(all_dst[:, 0]).reshape(1, BLOCKS), "efT": efT, "att": att,
        "W_rel": asn(L0_gnn_W_rel), "W_relT": asn(np.asarray(L0_gnn_W_rel).transpose(0, 2, 1)),
        "W_self": asn(L0_gnn_W_self), "W_selfT": asn(np.asarray(L0_gnn_W_self).T),
        "W_cross": asn(L0_gnn_W_cross), "W_crossT": asn(np.asarray(L0_gnn_W_cross).T),
        "bias_rel": asn(L0_gnn_bias_rel), "bias_lang": asn(L0_gnn_bias_lang),
        "We1": asn(L1_gnn_We1), "We2": asn(L1_gnn_We2), "Wn1": asn(L1_gnn_Wn1), "Wn2": asn(L1_gnn_Wn2),
    }
    T = Namespace()
    for name, a in given.items():
        T.__dict__[name] = nc.dram_tensor(f"in_{name}", a.shape, mybir.dt.from_np(a.dtype), kind="ExternalInput").ap()
    inner = lambda name, shape, dt=F32: nc.dram_tensor(name, shape, dt, kind="Internal").ap()
    T.sched_w, T.sched_e = inner("sched_w", (P * KC,), I32), inner("sched_e", (P * KC,), I32)
    T.xrel, T.esrc, T.srow = inner("xrel", (R * NP, XR)), inner("esrc", (R * NP, H)), inner("srow", (NP, C + 2 * H))
    T.edm, T.valid = inner("edm", (NP, R * 2 * H)), inner("valid", (NP, R))
    T.x1, T.ab = inner("x1", (NP, C)), inner("ab", (NP, 2 * HID))
    T.sums = [inner(f"sums{q}", (SUM_ROWS, HID)) for q in range(2)]
    T.out = nc.dram_tensor("out", (NP, C), F32, kind="ExternalOutput").ap()
    build(nc, T)
    r = run(nc, [{f"in_{k}": a for k, a in given.items()}], core_ids=[0])
    return r.results[0]["out"][:N_NODES]
```
